# Optimizing a Trainium2 kernel written in Bass

```python
import numpy as np
import jax
import jax.numpy as jnp

def _softmax(x, axis=-1):
    return jax.nn.softmax(x, axis=axis)

def _gelu(x):
    return jax.nn.gelu(x, approximate=True)

def _silu(x):
    return jax.nn.silu(x)

def _sigmoid(x):
    return jax.nn.sigmoid(x)

def _layernorm(x, axis=-1, eps=1e-05):
    m = jnp.mean(x, axis=axis, keepdims=True)
    v = jnp.var(x, axis=axis, keepdims=True)
    return (x - m) / jnp.sqrt(v + eps)

def _scatter_add(tgt, idx, src, axis=0):
    return tgt.at[idx].add(src)

def _segment_sum(src, seg, n):
    return jax.ops.segment_sum(src, seg, n)
kernel_name = 'mk_xattn_ffn_d1_seqx_r4_cbab4f'

def setup_inputs(seed: int=0):
    np.random.seed(seed)
    _w = jnp.asarray

    def _rec_inputs():
        import jax
        import jax.numpy as jnp
        _rk = jax.random.key(seed)
        x = 4.136e-05 + 0.9999 * jax.random.normal(jax.random.fold_in(_rk, 1), (4, 512, 512), jnp.float32)
        _lenS = 512 - jax.random.randint(jax.random.fold_in(_rk, 7), (4,), 0, max(1, 512 // 4) + 1, jnp.int32)
        _lenS2 = 512 - jax.random.randint(jax.random.fold_in(_rk, 8), (4,), 0, max(1, 512 // 4) + 1, jnp.int32)
        _ctx_1024P = jax.random.normal(jax.random.fold_in(_rk, 11), (4, 16, 256), jnp.float32)
        _ctx_1024c = jax.random.dirichlet(jax.random.fold_in(_rk, 511), 0.3 * jnp.ones((16,), jnp.float32), (4, 512))
        _ctx_1024t = jnp.einsum('bsk,bkd->bsd', _ctx_1024c, _ctx_1024P)
        _ctx_1024t = _ctx_1024t * jax.lax.rsqrt(jnp.mean(jnp.square(_ctx_1024t)) + 1e-12) * 0.953939
        ctx_1024 = -0.000292821 + 1.00034 * (_ctx_1024t + 0.3 * jax.random.normal(jax.random.fold_in(_rk, 611), (4, 512, 256), jnp.float32))
        return (x, ctx_1024)
    x, ctx_1024 = _rec_inputs()

    def _L0_xattn_setup():
        import jax, jax.numpy as jnp
        import numpy as np
        import math
        B, L, DM = (2, 512, 256)
        DS, DC, EXP = (16, 4, 2)
        DI = EXP * DM
        DR = math.ceil(DM / 16)
        DT_MIN, DT_MAX, DT_FLOOR = (0.001, 0.1, 0.0001)

        def _ssm_forward(hidden_states, z, in_proj_w, conv_w, conv_b, x_proj_w, dt_proj_w, dt_proj_b, A_log, D):
            b = hidden_states.shape[0]
            x = jnp.einsum('ed,bld->bel', in_proj_w, hidden_states)
            xp = jnp.pad(x, ((0, 0), (0, 0), (DC - 1, 0)))
            xc = jax.lax.conv_general_dilated(xp, conv_w[:, None, :], window_strides=(1,), padding='VALID', dimension_numbers=('NCH', 'OIH', 'NCH'), feature_group_count=DI)
            u = jax.nn.silu(xc + conv_b[None, :, None])
            x_dbl = jnp.einsum('ke,bel->bkl', x_proj_w, u)
            dt_lo = x_dbl[:, :DR]
            Bm = x_dbl[:, DR:DR + DS]
            Cm = x_dbl[:, DR + DS:]
            delta = jax.nn.softplus(jnp.einsum('er,brl->bel', dt_proj_w, dt_lo) + dt_proj_b[None, :, None])
            A = -jnp.exp(A_log)

            def step(state, xs):
                d_t, B_t, C_t, u_t = xs
                dA = jnp.exp(d_t[..., None] * A)
                state = state * dA + (d_t * u_t)[..., None] * B_t[:, None, :]
                y_t = jnp.einsum('ben,bn->be', state, C_t)
                return (state, y_t)
            xs = (jnp.moveaxis(delta, -1, 0), jnp.moveaxis(Bm, -1, 0), jnp.moveaxis(Cm, -1, 0), jnp.moveaxis(u, -1, 0))
            state0 = jnp.zeros((b, DI, DS), delta.dtype)
            _, ys = jax.lax.scan(step, state0, xs)
            y = jnp.moveaxis(ys, 0, -1)
            y = y + D[None, :, None] * u
            y = y * jax.nn.silu(z)
            return jnp.swapaxes(y, 1, 2)
        key = jax.random.key(seed)
        ks = jax.random.split(key, 8)
        hidden_states = jax.random.normal(ks[0], (B, L, DM), jnp.float32)
        z = jax.random.normal(ks[1], (B, DI, L), jnp.float32)
        in_proj_w = jax.random.normal(ks[2], (DI, DM), jnp.float32) * DM ** (-0.5)
        conv_w = jax.random.normal(ks[3], (DI, DC), jnp.float32) * DC ** (-0.5)
        conv_b = jnp.zeros((DI,), jnp.float32)
        x_proj_w = jax.random.normal(ks[4], (DR + 2 * DS, DI), jnp.float32) * DI ** (-0.5)
        dt_std = DR ** (-0.5)
        dt_proj_w = jax.random.uniform(ks[5], (DI, DR), jnp.float32, -dt_std, dt_std)
        dt = jnp.exp(jax.random.uniform(ks[6], (DI,), jnp.float32) * (math.log(DT_MAX) - math.log(DT_MIN)) + math.log(DT_MIN))
        dt = jnp.clip(dt, DT_FLOOR)
        dt_proj_b = dt + jnp.log(-jnp.expm1(-dt))
        A_log = jnp.log(jnp.broadcast_to(jnp.arange(1, DS + 1, dtype=jnp.float32), (DI, DS)))
        D = jnp.ones((DI,), jnp.float32)
        return dict(hidden_states=hidden_states, z=z, in_proj_w=in_proj_w, conv_w=conv_w, conv_b=conv_b, x_proj_w=x_proj_w, dt_proj_w=dt_proj_w, dt_proj_b=dt_proj_b, A_log=A_log, D=D)
    _L0_xattn_all = _L0_xattn_setup()
    _L0_xattn_in = {k: v for k, v in _L0_xattn_all.items() if k in ('in_proj_w', 'conv_w', 'conv_b', 'x_proj_w', 'dt_proj_w', 'dt_proj_b', 'A_log', 'D')}
    del _L0_xattn_all

    def _L0_ffn_setup():
        import math
        import jax, jax.numpy as jnp
        import numpy as np
        DIM = 512
        RANK = 8
        B, T = (4, 1024)

        def _orthogonal(key, n):
            a = jax.random.normal(key, (n, n), dtype=jnp.float32)
            q, r = jnp.linalg.qr(a)
            q = q * jnp.sign(jnp.diagonal(r))[None, :]
            return q
        key = jax.random.key(seed)
        kx, kf = jax.random.split(key)
        x = jax.random.normal(kx, (B, T, DIM), dtype=jnp.float32)
        fkeys = jax.random.split(kf, RANK)
        factors = jnp.stack([_orthogonal(fkeys[r], DIM) * (r + 1) ** (-0.5) for r in range(RANK)])
        bias = jnp.zeros((DIM,), dtype=jnp.float32)
        return {'x': x, 'factors': factors, 'bias': bias}
    _L0_ffn_all = _L0_ffn_setup()
    _L0_ffn_in = {k: v for k, v in _L0_ffn_all.items() if k in ('factors', 'bias')}
    del _L0_ffn_all
    return {'x': x, 'ctx_1024': ctx_1024, 'L0_xattn_in_proj_w': _L0_xattn_in['in_proj_w'], 'L0_xattn_conv_w': _L0_xattn_in['conv_w'], 'L0_xattn_conv_b': _L0_xattn_in['conv_b'], 'L0_xattn_x_proj_w': _L0_xattn_in['x_proj_w'], 'L0_xattn_dt_proj_w': _L0_xattn_in['dt_proj_w'], 'L0_xattn_dt_proj_b': _L0_xattn_in['dt_proj_b'], 'L0_xattn_A_log': _L0_xattn_in['A_log'], 'L0_xattn_D': _L0_xattn_in['D'], 'L0_ffn_factors': _L0_ffn_in['factors'], 'L0_ffn_bias': _L0_ffn_in['bias']}

def reference(x, ctx_1024, L0_xattn_in_proj_w, L0_xattn_conv_w, L0_xattn_conv_b, L0_xattn_x_proj_w, L0_xattn_dt_proj_w, L0_xattn_dt_proj_b, L0_xattn_A_log, L0_xattn_D, L0_ffn_factors, L0_ffn_bias):
    import jax
    import jax.numpy as jnp

    def _L0_xattn_ref(hidden_states, z, in_proj_w, conv_w, conv_b, x_proj_w, dt_proj_w, dt_proj_b, A_log, D):
        import jax, jax.numpy as jnp
        import numpy as np
        import math
        B, L, DM = (2, 512, 256)
        DS, DC, EXP = (16, 4, 2)
        DI = EXP * DM
        DR = math.ceil(DM / 16)
        DT_MIN, DT_MAX, DT_FLOOR = (0.001, 0.1, 0.0001)

        def _ssm_forward(hidden_states, z, in_proj_w, conv_w, conv_b, x_proj_w, dt_proj_w, dt_proj_b, A_log, D):
            b = hidden_states.shape[0]
            x = jnp.einsum('ed,bld->bel', in_proj_w, hidden_states)
            xp = jnp.pad(x, ((0, 0), (0, 0), (DC - 1, 0)))
            xc = jax.lax.conv_general_dilated(xp, conv_w[:, None, :], window_strides=(1,), padding='VALID', dimension_numbers=('NCH', 'OIH', 'NCH'), feature_group_count=DI)
            u = jax.nn.silu(xc + conv_b[None, :, None])
            x_dbl = jnp.einsum('ke,bel->bkl', x_proj_w, u)
            dt_lo = x_dbl[:, :DR]
            Bm = x_dbl[:, DR:DR + DS]
            Cm = x_dbl[:, DR + DS:]
            delta = jax.nn.softplus(jnp.einsum('er,brl->bel', dt_proj_w, dt_lo) + dt_proj_b[None, :, None])
            A = -jnp.exp(A_log)

            def step(state, xs):
                d_t, B_t, C_t, u_t = xs
                dA = jnp.exp(d_t[..., None] * A)
                state = state * dA + (d_t * u_t)[..., None] * B_t[:, None, :]
                y_t = jnp.einsum('ben,bn->be', state, C_t)
                return (state, y_t)
            xs = (jnp.moveaxis(delta, -1, 0), jnp.moveaxis(Bm, -1, 0), jnp.moveaxis(Cm, -1, 0), jnp.moveaxis(u, -1, 0))
            state0 = jnp.zeros((b, DI, DS), delta.dtype)
            _, ys = jax.lax.scan(step, state0, xs)
            y = jnp.moveaxis(ys, 0, -1)
            y = y + D[None, :, None] * u
            y = y * jax.nn.silu(z)
            return jnp.swapaxes(y, 1, 2)
        return _ssm_forward(hidden_states, z, in_proj_w, conv_w, conv_b, x_proj_w, dt_proj_w, dt_proj_b, A_log, D)

    def _L0_ffn_ref(x, factors, bias):
        import math
        import jax, jax.numpy as jnp
        import numpy as np
        DIM = 512
        RANK = 8
        B, T = (4, 1024)

        def _orthogonal(key, n):
            a = jax.random.normal(key, (n, n), dtype=jnp.float32)
            q, r = jnp.linalg.qr(a)
            q = q * jnp.sign(jnp.diagonal(r))[None, :]
            return q
        rank = factors.shape[0]
        mixed = jnp.einsum('btd,rde->bte', x, factors)
        mixed = mixed / math.sqrt(rank) + bias
        return mixed
    x = x + _L0_xattn_ref(ctx_1024, _layernorm(x, axis=-1), L0_xattn_in_proj_w, L0_xattn_conv_w, L0_xattn_conv_b, L0_xattn_x_proj_w, L0_xattn_dt_proj_w, L0_xattn_dt_proj_b, L0_xattn_A_log, L0_xattn_D)
    x = x + _L0_ffn_ref(_layernorm(x, axis=-1), L0_ffn_factors, L0_ffn_bias)
    return x

_drawn_inputs = setup_inputs


def setup_inputs(seed=0):
    import zlib

    import numpy as np

    out = dict(_drawn_inputs(seed))
    spreads = {'L0_xattn_conv_b': (0.0, 0.1), 'L0_xattn_D': (1.0, 0.2), 'L0_ffn_bias': (0.0, 0.1)}
    factors = {'L0_xattn_dt_proj_w': 5.28}
    for name, (base, spread) in spreads.items():
        noise = np.random.default_rng([zlib.crc32(name.encode()), seed]).standard_normal(out[name].shape)
        drawn = base * np.exp(spread * noise) if base else spread * noise
        out[name] = jnp.asarray(drawn.astype(out[name].dtype))
    for name, factor in factors.items():
        out[name] = (out[name] * factor).astype(out[name].dtype)
    return out
```

```python
from contextlib import ExitStack

import concourse.bass as bass
from concourse import mybir

ALU = mybir.AluOpType
ACT = mybir.ActivationFunctionType
F32 = mybir.dt.float32

P = 128
LN_EXP = "natural_log_exp_and_others"
LN_EPS = 1e-5
SOFTPLUS_LINEAR = 30.0


def plan(batches, tiles, pairs):
    def project(b, part):
        if not 0 <= b < batches:
            return []
        if part == 0:
            return [("conv", b, e) for e in range(tiles)]
        return [("xproj", b, 0), ("bt", b, 0)] + [("dt", b, e) for e in range(tiles)] + [("dut", b, e) for e in range(tiles)]

    def feed(b, half):
        if not 0 <= b < batches:
            return []
        js = range(half * tiles // 2, (half + 1) * tiles // 2)
        return [("yt", b, j) for j in js] + [("ht", b, j) for j in js] + [("ffn", b, j) for j in js]

    steps = {-1: [[], project(0, 0) + project(0, 1)]}
    for b in range(batches):
        steps[b] = [[("gate", b - 1, e) for e in range(tiles)] if b else [],
                    feed(b - 1, 0) + feed(b - 1, 1), project(b + 1, 0), project(b + 1, 1)]
    steps[batches] = [[("gate", batches - 1, e) for e in range(tiles)], feed(batches - 1, 0) + feed(batches - 1, 1)]
    return steps


def ssm_ffn_kernel(nc, x, ctxT, winT, per_channel, xprojT, dtprojT, factors, ffn_bias, identity, out):
    NB, L, DI = x.shape
    DM = ctxT.shape[1]
    R = xprojT.shape[1]
    DR = dtprojT.shape[0]
    NS = (R - DR) // 2
    DC = per_channel.shape[2] - NS - 3
    RANK = factors.shape[0]
    ET = DI // P
    TT = L // P
    KT = DM // P
    FFN_SCALE = float(RANK) ** -0.5
    assert L == DI == 512 and NS % 4 == 0 and ET == TT == 4

    UB = NS * ET
    PAIRS = NS // 2
    SEGMENTS = [(0, 1), (1, 3), (3, 6), (6, 8)]
    assert SEGMENTS[-1][1] == PAIRS
    SDBU = 2
    SDA = 8
    SST = 4
    SPR = 8
    steps = plan(NB, ET, PAIRS)
    in_psum = [s for k in sorted(steps) for part in steps[k] for s in part if s[0] != "gate"]
    use = {s: q for q, s in enumerate(in_psum)}

    with ExitStack() as ctx:
        def sb(name, shape):
            return ctx.enter_context(nc.sbuf_tensor(name, shape, F32))

        def sem(name):
            return ctx.enter_context(nc.semaphore(name))

        ident = sb("ident", [P, P])
        w_in = sb("w_in", [P, KT, DI])
        w_xp = sb("w_xp", [P, ET, R])
        w_dt = sb("w_dt", [DR, DI])
        chan = sb("chan", [P, ET, DC + 3 + NS])
        taps = chan[:, :, 0:DC]
        b_conv, b_dt, skip = (chan[:, :, DC + i] for i in range(3))
        a_log = chan[:, :, DC + 3:]
        a_neg = sb("a_neg", [P, ET, NS])
        bias_row = sb("bias_row", [P, DI])
        eps = sb("eps", [P, 1])
        w_ffn = sb("w_ffn", [P, ET, DI])
        xin = sb("xin", [P, 2, ET, L])
        u = sb("u", [P, 2, ET, L])
        delta = sb("delta", [P, 2, ET, L])
        work = sb("work", [P, ET, L])
        zs = sb("zs", [P, 2, ET, L])
        xdbl = sb("xdbl", [R, L])
        bt = sb("bt", [P, 2, TT, R])
        du_t = sb("du_t", [P, 2, TT, DI])
        c_row = sb("c_row", [P, NS, L])
        stats = sb("stats", [P, ET, 6])
        mv = sb("mv", [P, ET, 2])
        rstd = sb("rstd", [P, ET])
        lnv = sb("lnv", [P, ET])
        nmr = sb("nmr", [P, ET])
        bx_t = sb("bx_t", [P, 2, TT, DI])
        decay = sb("decay", [P, SDA, L])
        state = sb("state", [P, SST, L])
        prod = sb("prod", [P, SPR, L])
        h = sb("h", [P, 2, DI])
        h_t = sb("h_t", [P, 2, ET, P])
        stats2 = sb("stats2", [P, 2, 6])
        mv2 = sb("mv2", [P, 2, 2])
        lnv2 = sb("lnv2", [P, 2])
        rstd2 = sb("rstd2", [P, 2])

        dbu = [ctx.enter_context(nc.psum_tensor(f"dbu{i}", [P, L], F32)) for i in range(SDBU)]
        acc = [ctx.enter_context(nc.psum_tensor(f"acc{i}", [P, L], F32)) for i in range(ET)]
        spare = [ctx.enter_context(nc.psum_tensor(f"spare{i}", [P, L], F32)) for i in range(2)]

        c_dram = nc.dram_tensor("c_scratch", [NB, NS, L], F32, kind="Internal").ap()

        w_proj_in = sem("w_proj_in")
        w_small_in = sem("w_small_in")
        ctx_in = sem("ctx_in")
        x_in = sem("x_in")
        f_in = [sem(f"f_in{i}") for i in range(2)]
        c_stored = sem("c_stored")
        c_in = [sem(f"c_in{i}") for i in range(len(SEGMENTS))]
        stored = sem("stored")
        f_added = sem("f_added")
        eps_set = sem("eps_set")
        a_exp = sem("a_exp")
        a_ready = sem("a_ready")
        projected = sem("projected")
        tap_now = sem("tap_now")
        tap_past = sem("tap_past")
        u_ready = sem("u_ready")
        z_stats = sem("z_stats")
        z_mv = sem("z_mv")
        z_ln = sem("z_ln")
        z_rstd = sem("z_rstd")
        z_nmr = sem("z_nmr")
        zs_ready = sem("zs_ready")
        xp_done = sem("xp_done")
        xd_ready = sem("xd_ready")
        bt_done = sem("bt_done")
        bt_ready = sem("bt_ready")
        dt_done = sem("dt_done")
        dt_capped = sem("dt_capped")
        dt_exp = sem("dt_exp")
        dt_ln = sem("dt_ln")
        delta_ready = sem("delta_ready")
        du_ready = sem("du_ready")
        dut_done = sem("dut_done")
        dut_ready = sem("dut_ready")
        bank_free = [sem(f"bank_free{i}") for i in range(2)]
        bx_ready = sem("bx_ready")
        decay_ready = sem("decay_ready")
        dbu_ready = sem("dbu_ready")
        pool_turn = sem("pool_turn")
        scanned = sem("scanned")
        multiplied = sem("multiplied")
        summed = sem("summed")
        y_skip = sem("y_skip")
        y_gated = sem("y_gated")
        yt_done = sem("yt_done")
        x1_ready = sem("x1_ready")
        x1_stats = sem("x1_stats")
        x1_mv = sem("x1_mv")
        x1_ln = sem("x1_ln")
        x1_rstd = sem("x1_rstd")
        x1_biased = sem("x1_biased")
        h_ready = sem("h_ready")
        ht_done = sem("ht_done")
        ht_ready = sem("ht_ready")
        ffn_done = sem("ffn_done")
        out_ready = sem("out_ready")

        block = ctx.enter_context(nc.Block())

        @block.sync
        def _(sp):
            sp.dma_start(w_in[:], winT.rearrange("(k p) e -> p k e", p=P)).then_inc(w_proj_in, 16)
            sp.dma_start(zs[:, 0, 0:KT], ctxT[0].rearrange("(k p) t -> p k t", p=P)).then_inc(ctx_in, 16)
            sp.dma_start(chan[:], per_channel).then_inc(w_small_in, 16)
            sp.dma_start(xin[:, 0], x[0].rearrange("(k p) t -> p k t", p=P)).then_inc(x_in, 16)
            sp.dma_start(ident[:], identity).then_inc(w_proj_in, 16)
            sp.dma_start(w_xp[:], xprojT.rearrange("(k p) r -> p k r", p=P)).then_inc(w_proj_in, 16)
            sp.dma_start(w_dt[:], dtprojT).then_inc(w_proj_in, 16)
            sp.dma_start(bias_row[:], ffn_bias.rearrange("(o e) -> o e", o=1).broadcast_to([P, DI])).then_inc(
                w_small_in, 16)
            for r in range(RANK):
                if r >= 2:
                    sp.wait_ge(f_added, r - 1)
                sp.dma_start(prod[:, 4 * (r % 2):4 * (r % 2) + 4],
                             factors[r].rearrange("(k p) e -> p k e", p=P)).then_inc(f_in[r % 2], 16)

            def load_c(b):
                sp.wait_ge(xd_ready, b + 1)
                sp.dma_start(c_dram[b], xdbl[DR + NS:R, :]).then_inc(c_stored, 16)
                sp.wait_ge(c_stored, 16 * (b + 1))
                for g, (p0, p1) in enumerate(SEGMENTS):
                    if b:
                        sp.wait_ge(multiplied, UB * (b - 1) + 2 * ET * p1)
                    rows = slice(2 * p0, 2 * p1)
                    sp.dma_start(c_row[:, rows], c_dram[b:b + 1, rows].broadcast_to([P, 2 * (p1 - p0), L])
                                 ).then_inc(c_in[g], 16)

            def store_out(b):
                for j in range(TT):
                    sp.wait_ge(out_ready, TT * b + j + 1)
                    sp.dma_start(out[b, j * P:(j + 1) * P, :], xin[:, b % 2, j]).then_inc(stored, 16)

            load_c(0)
            for b in range(NB):
                if b + 1 < NB:
                    if b:
                        sp.wait_ge(y_gated, ET * b)
                    sp.dma_start(zs[:, (b + 1) % 2, 0:KT], ctxT[b + 1].rearrange("(k p) t -> p k t", p=P)).then_inc(ctx_in, 16)
                if b:
                    store_out(b - 1)
                if b + 1 < NB:
                    if b:
                        sp.wait_ge(stored, 16 * TT * b)
                    sp.dma_start(xin[:, (b + 1) % 2], x[b + 1].rearrange("(k p) t -> p k t", p=P)).then_inc(x_in, 16)
                    load_c(b + 1)
            store_out(NB - 1)
            sp.wait_ge(stored, 16 * TT * NB)

        @block.gpsimd
        def _(pool):
            for r in range(1, RANK):
                if r == 1:
                    pool.wait_ge(f_in[0], 16)
                pool.wait_ge(f_in[r % 2], 16 * (r // 2 + 1))
                first = prod[:, 0:4] if r == 1 else w_ffn[:]
                if r > 1:
                    pool.wait_ge(f_added, r)
                nc.gpsimd.tensor_tensor(w_ffn[:], first, prod[:, 4 * (r % 2):4 * (r % 2) + 4], ALU.add).then_inc(
                    f_added, 2 if r == 1 else 1)

            pool.wait_ge(f_added, RANK)

            def states(b, g, n, odd):
                for e in range(ET):
                    unit = UB * b + ET * n + e
                    slot = 4 * odd + e
                    pool.wait_ge(scanned, unit + 1)
                    if not (isinstance(n, int) and b == 0 and n < 2):
                        pool.wait_ge(summed, unit - SPR + 1)
                    pool.wait_ge(c_in[g], 16 * (b + 1))
                    pool.sem_inc(pool_turn, 1)
                    nc.gpsimd.tensor_tensor(prod[:, slot], state[:, e], c_row[:, bass.ds(n, 1), :].rearrange(
                        "p o t -> p (o t)"), ALU.mult).then_inc(multiplied, 1)

            def stage(kind, b, j):
                if kind == "yt":
                    pool.wait_ge(x1_ready, TT * b + j + 1)
                    nc.gpsimd.tensor_tensor(xin[:, b % 2, j], h[:, j % 2], bias_row[:], ALU.add).then_inc(x1_biased, 1)

            for b in range(NB):
                for g, (p0, p1) in enumerate(SEGMENTS):
                    if g == 0:
                        states(b, g, 0, 0)
                        for s in steps[b][0]:
                            stage(*s)
                        states(b, g, 1, 1)
                    else:
                        with pool.Fori(p0, p1) as i:
                            states(b, g, i * 2, 0)
                            states(b, g, i * 2 + 1, 1)
                    if g < 3:
                        for s in steps[b][g + 1]:
                            stage(*s)
            for s in steps[NB][1]:
                stage(*s)

        @block.scalar
        def _(act):
            def copy_conv(b, e):
                k = ET * b + e
                act.wait_ge(projected, k + 1)
                if e == 0 and b:
                    act.wait_ge(dut_done, ET * b)
                nc.scalar.activation(work[:, e], spare[use["conv", b, e] % 2][:], ACT.Copy,
                                     scale=taps[:, e, DC - 1:DC]).then_inc(tap_now, 1)

            def silus(b):
                nc.scalar.preload_act_table_set(LN_EXP)
                act.wait_ge(z_mv, ET * (b + 1))
                nc.scalar.activation(lnv[:], mv[:, :, 1], ACT.Ln, bias=eps[:, 0:1]).then_inc(z_ln, 1)
                act.wait_ge(z_ln, b + 1)
                nc.scalar.activation(rstd[:], lnv[:], ACT.Exp, scale=-0.5).then_inc(z_rstd, 1)
                for e in range(ET):
                    act.wait_ge(tap_past, (DC - 1) * (ET * b + (e | 1) + 1))
                    if e == 0 and b >= 2:
                        act.wait_ge(yt_done, TT * (b - 1))
                    nc.scalar.activation(u[:, b % 2, e], work[:, e], ACT.Silu, bias=b_conv[:, e:e + 1]).then_inc(
                        u_ready, 1)
                act.wait_ge(z_nmr, b + 1)
                act.wait_ge(projected, ET * (b + 1))
                if b >= 2:
                    act.wait_ge(y_gated, ET * (b - 1))
                for e in range(ET):
                    nc.scalar.activation(zs[:, b % 2, e], xin[:, b % 2, e], ACT.Silu, scale=rstd[:, e:e + 1],
                                         bias=nmr[:, e:e + 1]).then_inc(zs_ready, 1)

            def stage(kind, b, j):
                k = ET * b + j
                if kind == "conv":
                    copy_conv(b, j)
                    if j == ET - 1:
                        silus(b)
                elif kind == "bt":
                    act.wait_ge(bt_done, b + 1)
                    q = use[kind, b, j]
                    nc.scalar.copy(bt[:, b % 2], spare[q % 2][:, 0:TT * R].rearrange("p (j r) -> p j r", r=R)
                                   ).then_inc(bt_ready, 1)
                    act.wait_ge(bt_ready, b + 1)
                    act.sem_inc(bank_free[q % 2], 1)
                elif kind == "dt":
                    if j == 0:
                        nc.scalar.preload_act_table_set(LN_EXP)
                    act.wait_ge(dt_capped, k + 1)
                    nc.scalar.activation(delta[:, b % 2, j], delta[:, b % 2, j], ACT.Exp).then_inc(dt_exp, 1)
                    act.wait_ge(dt_exp, k + 1)
                    nc.scalar.activation(delta[:, b % 2, j], delta[:, b % 2, j], ACT.Ln, bias=1.0).then_inc(dt_ln, 1)
                elif kind == "dut":
                    act.wait_ge(dut_done, k + 1)
                    q = use[kind, b, j]
                    nc.scalar.copy(du_t[:, b % 2, :, j * P:(j + 1) * P],
                                   spare[q % 2][:].rearrange("p (j c) -> p j c", c=P)).then_inc(dut_ready, 1)
                    act.wait_ge(dut_ready, k + 1)
                    act.sem_inc(bank_free[q % 2], 1)
                elif kind == "yt":
                    act.wait_ge(x1_mv, k + 1)
                    nc.scalar.activation(lnv2[:, j % 2:j % 2 + 1], mv2[:, j % 2, 1:2], ACT.Ln, bias=eps[:, 0:1]
                                         ).then_inc(x1_ln, 1)
                    act.wait_ge(x1_ln, k + 1)
                    if k >= 2:
                        act.wait_ge(h_ready, k - 1)
                    nc.scalar.activation(rstd2[:, j % 2:j % 2 + 1], lnv2[:, j % 2:j % 2 + 1], ACT.Exp, scale=-0.5
                                         ).then_inc(x1_rstd, 1)
                elif kind == "ht":
                    act.wait_ge(ht_done, k + 1)
                    q = use[kind, b, j]
                    if k >= 2:
                        act.wait_ge(ffn_done, k - 1)
                    nc.scalar.copy(h_t[:, j % 2], spare[q % 2][:].rearrange("p (k t) -> p k t", t=P)).then_inc(
                        ht_ready, 1)
                    act.wait_ge(ht_ready, k + 1)
                    act.sem_inc(bank_free[q % 2], 1)

            def states(b, n, odd):
                if not (isinstance(n, int) and b == 0 and n < 2):
                    act.wait_ge(dbu_ready, UB * b + ET * (n - 1))
                for j in range(TT):
                    nc.scalar.activation(bx_t[:, odd, j], du_t[:, b % 2, j], ACT.Copy,
                                         scale=bt[:, b % 2, j, bass.ds(n + DR, 1)]).then_inc(bx_ready, 1)
                for e in range(ET):
                    unit = UB * b + ET * n + e
                    if not (isinstance(n, int) and b == 0 and n < 2):
                        act.wait_ge(scanned, unit - SDA + 1)
                    nc.scalar.activation(decay[:, 4 * odd + e], delta[:, b % 2, e], ACT.Exp,
                                         scale=a_neg[:, e, bass.ds(n, 1)]).then_inc(decay_ready, 1)

            nc.scalar.preload_act_table_set(LN_EXP)
            act.wait_ge(w_small_in, 16 * 2)
            nc.scalar.activation(a_neg[:], a_log, ACT.Exp).then_inc(a_exp, 1)
            act.wait_ge(eps_set, 1)
            for s in steps[-1][1]:
                stage(*s)
            act.wait_ge(a_ready, 1)
            for b in range(NB):
                act.wait_ge(delta_ready, ET * (b + 1))
                act.wait_ge(dut_ready, ET * (b + 1))
                act.wait_ge(bt_ready, b + 1)
                for g, (p0, p1) in enumerate(SEGMENTS):
                    nc.scalar.preload_act_table_set(LN_EXP)
                    if g == 0:
                        states(b, 0, 0)
                        for s in steps[b][0]:
                            stage(*s)
                        states(b, 1, 1)
                    else:
                        with act.Fori(p0, p1) as i:
                            states(b, i * 2, 0)
                            states(b, i * 2 + 1, 1)
                    if g < 3:
                        for s in steps[b][g + 1]:
                            stage(*s)
            for s in steps[NB][1]:
                stage(*s)

        @block.vector
        def _(dve):
            def z_norm(b):
                dve.wait_ge(x_in, 16 * (b + 1))
                if b:
                    dve.wait_ge(zs_ready, ET * b)
                for e in range(ET):
                    nc.vector.bn_stats(stats[:, e], xin[:, b % 2, e]).then_inc(z_stats, 1)
                for e in range(ET):
                    dve.wait_ge(z_stats, ET * b + e + 1)
                    nc.vector.bn_aggr(mv[:, e], stats[:, e]).then_inc(z_mv, 1)

            def z_shift(b):
                dve.wait_ge(z_rstd, b + 1)
                dve.wait_ge(z_mv, ET * (b + 1))
                nc.vector.scalar_tensor_tensor(out=nmr[:], in0=mv[:, :, 0], scalar=-1.0, in1=rstd[:], op0=ALU.mult,
                                               op1=ALU.mult).then_inc(z_nmr, 1)

            def conv(b, pair):
                for s in range(1, DC):
                    for e in pair:
                        k = ET * b + e
                        if s == 1:
                            dve.wait_ge(tap_now, k + 1)
                        else:
                            dve.wait_ge(tap_past, (DC - 1) * (ET * b + pair[0]) + 2 * (s - 2) + (e - pair[0]) + 1)
                        q = use["conv", b, e]
                        last = nc.vector.scalar_tensor_tensor(
                            out=work[:, e, s:], in0=spare[q % 2][:, :L - s], scalar=taps[:, e, DC - 1 - s:DC - s],
                            in1=work[:, e, s:], op0=ALU.mult, op1=ALU.add).then_inc(tap_past, 1)
                dve.wait_ge(tap_past, (DC - 1) * (ET * b + pair[-1] + 1))
                for e in pair:
                    dve.sem_inc(bank_free[use["conv", b, e] % 2], 1)

            def stage(kind, b, j):
                k = ET * b + j
                if kind == "conv":
                    if j == 0:
                        z_norm(b)
                    if j % 2:
                        conv(b, (j - 1, j))
                    if j == ET - 1:
                        z_shift(b)
                elif kind == "xproj":
                    q = use[kind, b, j]
                    dve.wait_ge(xp_done, b + 1)
                    if b:
                        dve.wait_ge(c_stored, 16 * b)
                        dve.wait_ge(dt_done, ET * b)
                        dve.wait_ge(bt_done, b)
                    nc.vector.tensor_copy(xdbl[:], spare[q % 2][0:R, :]).then_inc(xd_ready, 1)
                    dve.wait_ge(xd_ready, b + 1)
                    dve.sem_inc(bank_free[q % 2], 1)
                elif kind == "dt":
                    q = use[kind, b, j]
                    dve.wait_ge(dt_done, k + 1)
                    if j == 0 and b >= 2:
                        dve.wait_ge(decay_ready, UB * (b - 1))
                    nc.vector.tensor_scalar(delta[:, b % 2, j], spare[q % 2][:], b_dt[:, j:j + 1], SOFTPLUS_LINEAR,
                                            ALU.add, ALU.min).then_inc(dt_capped, 1)
                    if j:
                        soft(b, j - 1)
                    if j == ET - 1:
                        soft(b, j)
                elif kind == "gate":
                    dve.wait_ge(summed, UB * (b + 1) - ET + j + 1)
                    nc.vector.scalar_tensor_tensor(out=u[:, b % 2, j], in0=u[:, b % 2, j], scalar=skip[:, j:j + 1],
                                                   in1=acc[j][:], op0=ALU.mult, op1=ALU.add).then_inc(y_skip, 1)
                    dve.wait_ge(y_skip, k + 1)
                    dve.wait_ge(zs_ready, ET * (b + 1))
                    nc.vector.tensor_tensor(u[:, b % 2, j], u[:, b % 2, j], zs[:, b % 2, j], ALU.mult).then_inc(y_gated, 1)
                elif kind == "yt":
                    q = use[kind, b, j]
                    dve.wait_ge(yt_done, k + 1)
                    if k >= 2:
                        dve.wait_ge(ht_done, k - 1)
                    nc.vector.tensor_tensor(h[:, j % 2], xin[:, b % 2, j], spare[q % 2][:], ALU.add).then_inc(
                        x1_ready, 1)
                    dve.wait_ge(x1_ready, k + 1)
                    dve.sem_inc(bank_free[q % 2], 1)
                    nc.vector.bn_stats(stats2[:, j % 2], h[:, j % 2]).then_inc(x1_stats, 1)
                    dve.wait_ge(x1_stats, k + 1)
                    if k >= 2:
                        dve.wait_ge(x1_ln, k - 1)
                    nc.vector.bn_aggr(mv2[:, j % 2], stats2[:, j % 2]).then_inc(x1_mv, 1)
                    dve.wait_ge(x1_rstd, k + 1)
                    dve.wait_ge(x1_biased, k + 1)
                    nc.vector.tensor_scalar(h[:, j % 2], h[:, j % 2], mv2[:, j % 2, 0:1], rstd2[:, j % 2:j % 2 + 1],
                                            ALU.subtract, ALU.mult).then_inc(h_ready, 1)
                elif kind == "ffn":
                    q = use[kind, b, j]
                    dve.wait_ge(ffn_done, k + 1)
                    dve.wait_ge(x1_biased, k + 1)
                    nc.vector.scalar_tensor_tensor(out=xin[:, b % 2, j], in0=spare[q % 2][:], scalar=FFN_SCALE,
                                                   in1=xin[:, b % 2, j], op0=ALU.mult, op1=ALU.add).then_inc(
                                                       out_ready, 1)
                    dve.wait_ge(out_ready, k + 1)
                    dve.sem_inc(bank_free[q % 2], 1)

            def soft(b, j):
                k = ET * b + j
                q = use["dt", b, j]
                dve.wait_ge(dt_ln, k + 1)
                nc.vector.scalar_tensor_tensor(out=delta[:, b % 2, j], in0=spare[q % 2][:], scalar=b_dt[:, j:j + 1],
                                               in1=delta[:, b % 2, j], op0=ALU.add, op1=ALU.max).then_inc(
                                                   delta_ready, 1)
                dve.wait_ge(delta_ready, k + 1)
                dve.sem_inc(bank_free[q % 2], 1)
                nc.vector.tensor_tensor(work[:, j], delta[:, b % 2, j], u[:, b % 2, j], ALU.mult).then_inc(du_ready, 1)

            def states(b, n, odd):
                for e in range(ET):
                    unit = UB * b + ET * n + e
                    dve.wait_ge(decay_ready, unit + 1)
                    dve.wait_ge(dbu_ready, unit + 1)
                    if not (isinstance(n, int) and b == 0 and n == 0):
                        dve.wait_ge(multiplied, unit - SST + 1)
                    nc.vector.tensor_tensor_scan(state[:, e], decay[:, 4 * odd + e], dbu[e % SDBU][:], 0.0, ALU.mult,
                                                 ALU.add).then_inc(scanned, 1)

            nc.vector.memset(eps[:], LN_EPS).then_inc(eps_set, 1)
            dve.wait_ge(w_small_in, 16 * 2)
            dve.wait_ge(a_exp, 1)
            nc.vector.tensor_scalar(a_neg[:], a_neg[:], -1.0, None, ALU.mult).then_inc(a_ready, 1)
            for s in steps[-1][1]:
                stage(*s)
            for b in range(NB):
                for g, (p0, p1) in enumerate(SEGMENTS):
                    if g == 0:
                        states(b, 0, 0)
                        for s in steps[b][0]:
                            stage(*s)
                        states(b, 1, 1)
                    else:
                        with dve.Fori(p0, p1) as i:
                            states(b, i * 2, 0)
                            states(b, i * 2 + 1, 1)
                    if g < 3:
                        for s in steps[b][g + 1]:
                            stage(*s)
            for s in steps[NB][0] + steps[NB][1]:
                stage(*s)

        @block.tensor
        def _(pe):
            def stage(kind, b, j):
                if kind == "gate":
                    return
                k = ET * b + j
                q = use[kind, b, j]
                bank = spare[q % 2]
                if q >= 2:
                    pe.wait_ge(bank_free[q % 2], q // 2)
                if kind == "conv":
                    if j == 0:
                        pe.wait_ge(ctx_in, 16 * (b + 1))
                    for c in range(KT):
                        last = nc.tensor.matmul(bank[:], w_in[:, c, j * P:(j + 1) * P], zs[:, b % 2, c], start=(c == 0),
                                                stop=(c == KT - 1))
                    last.then_inc(projected, 1)
                elif kind == "xproj":
                    for e in range(ET):
                        pe.wait_ge(u_ready, ET * b + e + 1)
                        last = nc.tensor.matmul(bank[0:R, :], w_xp[:, e], u[:, b % 2, e], start=(e == 0),
                                                stop=(e == ET - 1))
                    last.then_inc(xp_done, 1)
                elif kind == "bt":
                    pe.wait_ge(xd_ready, b + 1)
                    for t in range(TT):
                        last = nc.tensor.transpose(bank[:, t * R:(t + 1) * R], xdbl[:, t * P:(t + 1) * P],
                                                   ident[0:R, 0:R])
                    last.then_inc(bt_done, 1)
                elif kind == "dt":
                    pe.wait_ge(xd_ready, b + 1)
                    nc.tensor.matmul(bank[:], w_dt[:, j * P:(j + 1) * P], xdbl[0:DR, :], start=True,
                                     stop=True).then_inc(dt_done, 1)
                elif kind == "dut":
                    pe.wait_ge(du_ready, k + 1)
                    for t in range(TT):
                        last = nc.tensor.transpose(bank[:, t * P:(t + 1) * P], work[:, j, t * P:(t + 1) * P], ident[:])
                    last.then_inc(dut_done, 1)
                elif kind == "yt":
                    for e in range(ET):
                        pe.wait_ge(y_gated, ET * b + e + 1)
                        last = nc.tensor.transpose(bank[:, e * P:(e + 1) * P], u[:, b % 2, e, j * P:(j + 1) * P],
                                                   ident[:])
                    last.then_inc(yt_done, 1)
                elif kind == "ht":
                    pe.wait_ge(h_ready, k + 1)
                    for c in range(ET):
                        last = nc.tensor.transpose(bank[:, c * P:(c + 1) * P], h[:, j % 2, c * P:(c + 1) * P],
                                                   ident[:])
                    last.then_inc(ht_done, 1)
                elif kind == "ffn":
                    pe.wait_ge(ht_ready, k + 1)
                    pe.wait_ge(f_added, RANK)
                    for c in range(ET):
                        last = nc.tensor.matmul(bank[:], h_t[:, j % 2, c], w_ffn[:, c], start=(c == 0),
                                                stop=(c == ET - 1))
                    last.then_inc(ffn_done, 1)

            def states(b, n, odd, first=False, sums=True):
                for e in range(ET):
                    unit = UB * b + ET * n + e
                    if e == 0:
                        pe.wait_ge(bx_ready, UB * b + TT * (n + 1))
                    if not (isinstance(n, int) and b == 0 and n == 0 and e < SDBU):
                        pe.wait_ge(scanned, unit - SDBU + 1)
                    for t in range(TT):
                        last = nc.tensor.transpose(dbu[e % SDBU][:, t * P:(t + 1) * P],
                                                   bx_t[:, odd, t, e * P:(e + 1) * P], ident[:])
                    last.then_inc(dbu_ready, 1)
                    if sums:
                        add(b, n - 1, 1 - odd, e, start=first)

            def add(b, n, odd, e, start=False, stop=False):
                pe.wait_ge(multiplied, UB * b + ET * n + e + 1)
                if start and b:
                    pe.wait_ge(y_skip, ET * (b - 1) + e + 1)
                nc.tensor.matmul(acc[e][:], ident[:], prod[:, 4 * odd + e], start=start, stop=stop).then_inc(summed, 1)

            pe.wait_ge(w_proj_in, 16 * 4)
            for s in steps[-1][1]:
                stage(*s)
            for b in range(NB):
                for g, (p0, p1) in enumerate(SEGMENTS):
                    if g == 0:
                        states(b, 0, 0, sums=False)
                        states(b, 1, 1, first=True)
                    else:
                        with pe.Fori(p0, p1) as i:
                            states(b, i * 2, 0)
                            states(b, i * 2 + 1, 1)
                    if g == 3:
                        for e in range(ET):
                            add(b, NS - 1, 1, e, stop=True)
                    if g < 3:
                        for s in steps[b][g + 1]:
                            stage(*s)
            for s in steps[NB][1]:
                stage(*s)


_INS = ["x", "ctxT", "winT", "per_channel", "xprojT", "dtprojT", "factors", "ffn_bias", "identity"]


def kernel(x, ctx_1024, L0_xattn_in_proj_w, L0_xattn_conv_w, L0_xattn_conv_b, L0_xattn_x_proj_w, L0_xattn_dt_proj_w,
           L0_xattn_dt_proj_b, L0_xattn_A_log, L0_xattn_D, L0_ffn_factors, L0_ffn_bias):
    import numpy as np
    import concourse.bacc as bacc
    from concourse.bass_utils import run_bass_kernel_spmd

    channels = np.concatenate([L0_xattn_conv_w, np.reshape(L0_xattn_conv_b, (-1, 1)),
                               np.reshape(L0_xattn_dt_proj_b, (-1, 1)), np.reshape(L0_xattn_D, (-1, 1)),
                               L0_xattn_A_log], axis=1)
    arrays = dict(
        x=np.ascontiguousarray(x),
        ctxT=np.ascontiguousarray(np.transpose(ctx_1024, (0, 2, 1))),
        winT=np.ascontiguousarray(np.transpose(L0_xattn_in_proj_w)),
        per_channel=np.ascontiguousarray(channels.reshape(-1, P, channels.shape[1]).transpose(1, 0, 2)),
        xprojT=np.ascontiguousarray(np.transpose(L0_xattn_x_proj_w)),
        dtprojT=np.ascontiguousarray(np.transpose(L0_xattn_dt_proj_w)),
        factors=np.ascontiguousarray(L0_ffn_factors),
        ffn_bias=np.ascontiguousarray(L0_ffn_bias),
        identity=np.eye(P, dtype=np.float32),
    )
    nc = bacc.Bacc("TRN2", target_bir_lowering=False, num_devices=1)
    args = [nc.dram_tensor(n, arrays[n].shape, mybir.dt.from_np(arrays[n].dtype), kind="ExternalInput").ap()
            for n in _INS]
    out = nc.dram_tensor("out", x.shape, F32, kind="ExternalOutput").ap()
    ssm_ffn_kernel(nc, *args, out)
    r = run_bass_kernel_spmd(nc, [arrays], core_ids=[0])
    return r.results[0]["out"]
```

```python
from contextlib import ExitStack

import concourse.bass as bass
from concourse import mybir

ALU = mybir.AluOpType
ACT = mybir.ActivationFunctionType
F32 = mybir.dt.float32

P = 128
LN_EXP = "natural_log_exp_and_others"
LN_EPS = 1e-5
SOFTPLUS_LINEAR = 30.0


NEXT, OWN, LAST = 1, 0, -1
OFFSET = dict(conv=NEXT, usilu=NEXT, xproj=NEXT, bt=NEXT, dt=NEXT, soft=NEXT, dut=NEXT,
              zstat=OWN, zshift=OWN, gatesilu=OWN,
              skip=LAST, gate=LAST, yt=LAST, rstd=LAST, norm=LAST, bias=LAST, ht=LAST, ffn=LAST)
PE_POINTS = {0: [("conv", 0)], 1: [("conv", 1)], 5: [("yt", 0)], 6: [("yt", 1)], 7: [("yt", 2)], 8: [("yt", 3)],
             9: [("conv", 2)], 10: [("conv", 3)], 13: [("ht", 0)], 14: [("ht", 1)], 15: [("ffn", 0)],
             16: [("xproj", 0)], 17: [("ffn", 1)], 18: [("bt", 0)], 19: [("dt", 0)], 20: [("dt", 1)],
             21: [("dt", 2)], 22: [("dt", 3)], 23: [("ht", 2)], 24: [("ht", 3)], 25: [("ffn", 2)],
             26: [("ffn", 3)], 27: [("dut", 0)], 28: [("dut", 1)], 29: [("dut", 2)], 30: [("dut", 3)]}
ACT_POINTS = {2: [("conv", 0), ("conv", 1)], 9: [("rstd", 0), ("rstd", 1)], 10: [("rstd", 2), ("rstd", 3)],
              12: [("conv", 2), ("conv", 3)], 14: [("zshift", 0), ("usilu", 0), ("gatesilu", 0)], 15: [("ht", 0)],
              16: [("ht", 1)], 20: [("bt", 0)], 21: [("dt", 0)], 22: [("dt", 1)], 23: [("dt", 2)], 24: [("dt", 3)],
              25: [("ht", 2)], 26: [("ht", 3)], 28: [("dut", 0)], 29: [("dut", 1)], 30: [("dut", 2)],
              31: [("dut", 3)]}
DVE_POINTS = {1: [("skip", 0), ("skip", 1)], 2: [("skip", 2), ("skip", 3)], 3: [("conv", 0)],
              4: [("gate", e) for e in range(4)], 5: [("zstat", 0)], 6: [("yt", 0)], 7: [("yt", 1)], 8: [("yt", 2)],
              9: [("yt", 3)], 11: [("norm", 0), ("norm", 1)], 12: [("conv", 2)], 14: [("zshift", 0), ("norm", 2)],
              15: [("norm", 3)], 16: [("ffn", 0)], 17: [("xproj", 0)], 18: [("ffn", 1)], 20: [("dt", 0)],
              21: [("dt", 1)], 22: [("dt", 2)], 23: [("dt", 3), ("soft", 0)], 24: [("soft", 1)], 25: [("soft", 2)],
              26: [("soft", 3), ("ffn", 2)], 27: [("ffn", 3)]}
POOL_POINTS = {7: [("bias", 0)], 8: [("bias", 1)], 9: [("bias", 2)], 10: [("bias", 3)]}


def stages_at(points, step, point, batches):
    return [(kind, step + OFFSET[kind], j) for kind, j in points.get(point, ()) if 0 <= step + OFFSET[kind] < batches]


def ssm_ffn_kernel(nc, x, ctxT, winT, per_channel, xprojT, dtprojT, factors, ffn_bias, identity, out):
    NB, L, DI = x.shape
    DM = ctxT.shape[1]
    R = xprojT.shape[1]
    DR = dtprojT.shape[0]
    NS = (R - DR) // 2
    DC = per_channel.shape[2] - NS - 3
    RANK = factors.shape[0]
    ET = DI // P
    TT = L // P
    KT = DM // P
    FFN_SCALE = float(RANK) ** -0.5
    assert L == DI == 512 and NS % 4 == 0 and ET == TT == 4

    UB = NS * ET
    POINTS = UB // 2
    GROUPS = 4
    NG = NS // GROUPS
    SDBU = 2
    SDA = 2 * ET
    SST = ET
    SPR = 2 * ET
    WARM = 5
    F_EARLY = 5
    STEPS = range(-1, NB + 1)
    use = {}
    for b in STEPS:
        for point in range(POINTS):
            for s in stages_at(PE_POINTS, b, point, NB):
                use[s] = len(use)

    with ExitStack() as ctx:
        def sb(name, shape):
            return ctx.enter_context(nc.sbuf_tensor(name, shape, F32))

        def sem(name):
            return ctx.enter_context(nc.semaphore(name))

        ident = sb("ident", [P, P])
        w_in = sb("w_in", [P, KT, DI])
        w_xp = sb("w_xp", [P, ET, R])
        w_dt = sb("w_dt", [DR, DI])
        chan = sb("chan", [P, ET, DC + 3 + NS])
        taps = chan[:, :, 0:DC]
        b_conv, b_dt, skip = (chan[:, :, DC + i] for i in range(3))
        a_log = chan[:, :, DC + 3:]
        a_neg = sb("a_neg", [P, ET, NS])
        bias_row = sb("bias_row", [P, DI])
        eps = sb("eps", [P, 1])
        w_ffn = sb("w_ffn", [P, ET, DI])
        xin = sb("xin", [P, 2, ET, L])
        u = sb("u", [P, 2, ET, L])
        delta = sb("delta", [P, 2, ET, L])
        work = sb("work", [P, ET, L])
        ctx_t = sb("ctx_t", [P, KT, L])
        zs = sb("zs", [P, ET, L])
        xdbl = sb("xdbl", [R, L])
        bt = sb("bt", [P, 2, TT, R])
        du_t = sb("du_t", [P, 2, TT, DI])
        c_row = sb("c_row", [P, NS, L])
        stats = sb("stats", [P, ET, 6])
        mv = sb("mv", [P, ET, 2])
        rstd = sb("rstd", [P, ET])
        lnv = sb("lnv", [P, ET])
        nmr = sb("nmr", [P, ET])
        bx_t = sb("bx_t", [P, 2, TT, DI])
        decay = sb("decay", [P, SDA, L])
        state = sb("state", [P, SST, L])
        prod = sb("prod", [P, SPR, L])
        h = sb("h", [P, TT, DI])
        h_t = sb("h_t", [P, 2, ET, P])
        stats2 = sb("stats2", [P, TT, 6])
        mv2 = sb("mv2", [P, TT, 2])
        lnv2 = sb("lnv2", [P, TT])
        rstd2 = sb("rstd2", [P, TT])

        warm = state[:, 0]

        dbu = [ctx.enter_context(nc.psum_tensor(f"dbu{i}", [P, L], F32)) for i in range(SDBU)]
        acc = [ctx.enter_context(nc.psum_tensor(f"acc{i}", [P, L], F32)) for i in range(ET)]
        spare = [ctx.enter_context(nc.psum_tensor(f"spare{i}", [P, L], F32)) for i in range(2)]

        c_dram = nc.dram_tensor("c_scratch", [NB, NS, L], F32, kind="Internal").ap()

        w_proj_in = sem("w_proj_in")
        w_small_in = sem("w_small_in")
        ctx_in = sem("ctx_in")
        x_in = sem("x_in")
        f_in = [sem(f"f_in{i}") for i in range(2)]
        c_stored = sem("c_stored")
        c_in = [sem(f"c_in{i}") for i in range(GROUPS)]
        stored = sem("stored")
        f_added = sem("f_added")
        warm_set = sem("warm_set")
        eps_set = sem("eps_set")
        a_exp = sem("a_exp")
        a_ready = sem("a_ready")
        projected = sem("projected")
        tap_now = sem("tap_now")
        tap_past = sem("tap_past")
        u_ready = sem("u_ready")
        z_stats = sem("z_stats")
        z_mv = sem("z_mv")
        z_ln = sem("z_ln")
        z_rstd = sem("z_rstd")
        z_nmr = sem("z_nmr")
        zs_ready = sem("zs_ready")
        xp_done = sem("xp_done")
        xd_ready = sem("xd_ready")
        bt_done = sem("bt_done")
        bt_ready = sem("bt_ready")
        dt_done = sem("dt_done")
        dt_biased = sem("dt_biased")
        dt_capped = sem("dt_capped")
        dt_exp = sem("dt_exp")
        dt_ln = sem("dt_ln")
        delta_ready = sem("delta_ready")
        du_ready = sem("du_ready")
        dut_done = sem("dut_done")
        dut_ready = sem("dut_ready")
        bank_free = [sem(f"bank_free{i}") for i in range(2)]
        bx_ready = sem("bx_ready")
        decay_ready = sem("decay_ready")
        dbu_ready = sem("dbu_ready")
        scanned = sem("scanned")
        multiplied = sem("multiplied")
        summed = sem("summed")
        y_skip = sem("y_skip")
        y_gated = sem("y_gated")
        yt_done = sem("yt_done")
        x1_ready = sem("x1_ready")
        x1_stats = sem("x1_stats")
        x1_mv = sem("x1_mv")
        x1_ln = sem("x1_ln")
        x1_rstd = sem("x1_rstd")
        x1_biased = sem("x1_biased")
        h_ready = sem("h_ready")
        ht_done = sem("ht_done")
        ht_ready = sem("ht_ready")
        ffn_done = sem("ffn_done")
        out_ready = sem("out_ready")

        block = ctx.enter_context(nc.Block())

        @block.sync
        def _(sp):
            sp.dma_start(w_in[:], winT.rearrange("(k p) e -> p k e", p=P)).then_inc(w_proj_in, 16)
            sp.dma_start(ctx_t[:], ctxT[0].rearrange("(k p) t -> p k t", p=P)).then_inc(ctx_in, 16)
            sp.dma_start(chan[:], per_channel).then_inc(w_small_in, 16)
            sp.dma_start(xin[:, 0], x[0].rearrange("(k p) t -> p k t", p=P)).then_inc(x_in, 16)
            sp.dma_start(ident[:], identity).then_inc(w_proj_in, 16)
            sp.dma_start(w_xp[:], xprojT.rearrange("(k p) r -> p k r", p=P)).then_inc(w_proj_in, 16)
            sp.dma_start(w_dt[:], dtprojT).then_inc(w_proj_in, 16)
            sp.dma_start(bias_row[:], ffn_bias.rearrange("(o e) -> o e", o=1).broadcast_to([P, DI])).then_inc(
                w_small_in, 16)
            sp.dma_start(xin[:, 1], x[1].rearrange("(k p) t -> p k t", p=P)).then_inc(x_in, 16)

            def load_factor(r):
                if r >= 2:
                    sp.wait_ge(f_added, max(ET * (r - 2), ET))
                sp.dma_start((zs, h)[r % 2][:], factors[r].rearrange("(k p) e -> p k e", p=P)).then_inc(f_in[r % 2], 16)

            for r in range(F_EARLY):
                load_factor(r)

            def load_c(b):
                sp.wait_ge(xd_ready, b + 1)
                sp.dma_start(c_dram[b], xdbl[DR + NS:R, :]).then_inc(c_stored, 16)
                sp.wait_ge(c_stored, 16 * (b + 1))
                for g in range(GROUPS):
                    rows = slice(NG * g, NG * (g + 1))
                    if b:
                        sp.wait_ge(multiplied, UB * (b - 1) + ET * NG * (g + 1))
                    sp.dma_start(c_row[:, rows], c_dram[b:b + 1, rows].broadcast_to([P, NG, L])).then_inc(c_in[g], 16)

            def load_x(b):
                if b >= 2:
                    sp.wait_ge(stored, 16 * TT * (b - 1))
                sp.dma_start(xin[:, b % 2], x[b].rearrange("(k p) t -> p k t", p=P)).then_inc(x_in, 16)

            def store_out(b, tiles):
                for j in tiles:
                    sp.wait_ge(out_ready, TT * b + j + 1)
                    sp.dma_start(out[b, j * P:(j + 1) * P, :], xin[:, b % 2, j]).then_inc(stored, 16)

            def load_context(b):
                sp.wait_ge(projected, ET * b)
                sp.dma_start(ctx_t[:], ctxT[b].rearrange("(k p) t -> p k t", p=P)).then_inc(ctx_in, 16)

            load_context(1)
            load_c(0)
            for r in range(F_EARLY, RANK):
                load_factor(r)
            for b in range(NB):
                if b:
                    store_out(b - 1, range(TT))
                    if b + 1 < NB:
                        load_x(b + 1)
                if b + 2 < NB:
                    load_context(b + 2)
                if b + 1 < NB:
                    load_c(b + 1)
            store_out(NB - 1, range(TT))
            sp.wait_ge(stored, 16 * TT * NB)

        @block.gpsimd
        def _(pool):
            def add_factor(r, j):
                if r == 1:
                    pool.wait_ge(f_in[0], 16)
                else:
                    pool.wait_ge(f_added, ET * (r - 2) + j + 1)
                pool.wait_ge(f_in[r % 2], 16 * (r // 2 + 1))
                nc.gpsimd.tensor_tensor(w_ffn[:, j], zs[:, j] if r == 1 else w_ffn[:, j], (zs, h)[r % 2][:, j],
                                        ALU.add).then_inc(f_added, 1)

            def unit(b, n, e):
                k = UB * b + ET * n + e
                if e == 0 and n % NG == 0:
                    pool.wait_ge(c_in[n // NG], 16 * (b + 1))
                pool.wait_ge(scanned, k + 1)
                if k >= SPR:
                    pool.wait_ge(summed, k - SPR + 1)
                nc.gpsimd.tensor_tensor(prod[:, k % SPR], state[:, e], c_row[:, n], ALU.mult).then_inc(multiplied, 1)

            def stage(kind, b, j):
                if kind == "bias":
                    pool.wait_ge(x1_ready, TT * b + j + 1)
                    nc.gpsimd.tensor_tensor(xin[:, b % 2, j], h[:, j], bias_row[:], ALU.add).then_inc(x1_biased, 1)

            for b in STEPS:
                for point in range(POINTS):
                    if 0 <= b < NB:
                        for k in (2 * point, 2 * point + 1):
                            unit(b, k // ET, k % ET)
                        if b == 0 and ET * (F_EARLY - 1) + point < ET * (RANK - 1):
                            k = ET * (F_EARLY - 1) + point
                            add_factor(k // ET + 1, k % ET)
                    for s in stages_at(POOL_POINTS, b, point, NB):
                        stage(*s)
                if b < 0:
                    for r in range(1, F_EARLY):
                        for j in range(ET):
                            add_factor(r, j)

        @block.scalar
        def _(act):
            def copy_conv(b, e):
                k = ET * b + e
                act.wait_ge(projected, k + 1)
                if e == 0 and b:
                    act.wait_ge(dut_done, ET * b)
                nc.scalar.activation(work[:, e], spare[use["conv", b, e] % 2][:], ACT.Copy,
                                     scale=taps[:, e, DC - 1:DC]).then_inc(tap_now, 1)

            def stage(kind, b, j):
                k = ET * b + j
                if kind == "conv":
                    copy_conv(b, j)
                elif kind == "zshift":
                    act.wait_ge(z_mv, ET * (b + 1))
                    nc.scalar.activation(lnv[:], mv[:, :, 1], ACT.Ln, bias=eps[:, 0:1]).then_inc(z_ln, 1)
                    act.wait_ge(z_ln, b + 1)
                    nc.scalar.activation(rstd[:], lnv[:], ACT.Exp, scale=-0.5).then_inc(z_rstd, 1)
                elif kind == "usilu":
                    for e in range(ET):
                        act.wait_ge(tap_past, (DC - 1) * (ET * b + (e | 1) + 1))
                        if e == 0 and b >= 2:
                            act.wait_ge(yt_done, TT * (b - 1))
                        nc.scalar.activation(u[:, b % 2, e], work[:, e], ACT.Silu, bias=b_conv[:, e:e + 1]).then_inc(
                            u_ready, 1)
                    if b == 0:
                        nc.scalar.preload_act_table_set(LN_EXP)
                elif kind == "gatesilu":
                    act.wait_ge(z_nmr, b + 1)
                    if b == 0:
                        act.wait_ge(f_added, ET * (RANK - 1))
                    if b:
                        act.wait_ge(y_gated, ET * b)
                    for e in range(ET):
                        nc.scalar.activation(zs[:, e], xin[:, b % 2, e], ACT.Silu, scale=rstd[:, e:e + 1],
                                             bias=nmr[:, e:e + 1]).then_inc(zs_ready, 1)
                    nc.scalar.preload_act_table_set(LN_EXP)
                elif kind == "bt":
                    act.wait_ge(bt_done, b + 1)
                    q = use[kind, b, j]
                    nc.scalar.copy(bt[:, b % 2], spare[q % 2][:, 0:TT * R].rearrange("p (j r) -> p j r", r=R)
                                   ).then_inc(bt_ready, 1)
                    act.wait_ge(bt_ready, b + 1)
                    act.sem_inc(bank_free[q % 2], 1)
                elif kind == "dt":
                    act.wait_ge(dt_capped, k + 1)
                    nc.scalar.activation(work[:, j], work[:, j], ACT.Exp).then_inc(dt_exp, 1)
                    act.wait_ge(dt_exp, k + 1)
                    nc.scalar.activation(work[:, j], work[:, j], ACT.Ln, bias=1.0).then_inc(dt_ln, 1)
                elif kind == "dut":
                    act.wait_ge(dut_done, k + 1)
                    q = use[kind, b, j]
                    nc.scalar.copy(du_t[:, b % 2, :, j * P:(j + 1) * P],
                                   spare[q % 2][:].rearrange("p (j c) -> p j c", c=P)).then_inc(dut_ready, 1)
                    act.wait_ge(dut_ready, k + 1)
                    act.sem_inc(bank_free[q % 2], 1)
                elif kind == "rstd":
                    act.wait_ge(x1_mv, k + 1)
                    nc.scalar.activation(lnv2[:, j:j + 1], mv2[:, j, 1:2], ACT.Ln, bias=eps[:, 0:1]
                                         ).then_inc(x1_ln, 1)
                    act.wait_ge(x1_ln, k + 1)
                    if b:
                        act.wait_ge(h_ready, k - TT + 1)
                    nc.scalar.activation(rstd2[:, j:j + 1], lnv2[:, j:j + 1], ACT.Exp, scale=-0.5
                                         ).then_inc(x1_rstd, 1)
                elif kind == "ht":
                    act.wait_ge(ht_done, k + 1)
                    q = use[kind, b, j]
                    if k >= 2:
                        act.wait_ge(ffn_done, k - 1)
                    nc.scalar.copy(h_t[:, j % 2], spare[q % 2][:].rearrange("p (k t) -> p k t", t=P)).then_inc(
                        ht_ready, 1)
                    act.wait_ge(ht_ready, k + 1)
                    act.sem_inc(bank_free[q % 2], 1)

            def unit(b, n, e):
                k = UB * b + ET * n + e
                if e == 0:
                    if UB * b + ET * n >= 2 * ET:
                        act.wait_ge(dbu_ready, UB * b + ET * (n - 1))
                    for j in range(TT):
                        nc.scalar.activation(bx_t[:, n % 2, j], du_t[:, b % 2, j], ACT.Copy,
                                             scale=bt[:, b % 2, j, DR + n:DR + n + 1]).then_inc(bx_ready, 1)
                if k >= SDA:
                    act.wait_ge(scanned, k - SDA + 1)
                nc.scalar.activation(decay[:, k % SDA], delta[:, b % 2, e], ACT.Exp,
                                     scale=a_neg[:, e, n:n + 1]).then_inc(decay_ready, 1)

            nc.scalar.preload_act_table_set(LN_EXP)
            act.wait_ge(w_small_in, 16 * 2)
            nc.scalar.activation(a_neg[:], a_log, ACT.Exp).then_inc(a_exp, 1)
            act.wait_ge(eps_set, 1)
            for b in STEPS:
                if 0 <= b < NB:
                    act.wait_ge(a_ready, 1)
                    act.wait_ge(delta_ready, ET * (b + 1))
                    act.wait_ge(dut_ready, ET * (b + 1))
                    act.wait_ge(bt_ready, b + 1)
                for point in range(POINTS):
                    if 0 <= b < NB:
                        for k in (2 * point, 2 * point + 1):
                            unit(b, k // ET, k % ET)
                    for s in stages_at(ACT_POINTS, b, point, NB):
                        stage(*s)

        @block.vector
        def _(dve):
            def z_norm(b):
                dve.wait_ge(x_in, 16 * (b + 1))
                if b:
                    dve.wait_ge(zs_ready, ET * b)
                for e in range(ET):
                    nc.vector.bn_stats(stats[:, e], xin[:, b % 2, e]).then_inc(z_stats, 1)
                for e in range(ET):
                    dve.wait_ge(z_stats, ET * b + e + 1)
                    nc.vector.bn_aggr(mv[:, e], stats[:, e]).then_inc(z_mv, 1)

            def z_shift(b):
                dve.wait_ge(z_rstd, b + 1)
                dve.wait_ge(z_mv, ET * (b + 1))
                nc.vector.scalar_tensor_tensor(out=nmr[:], in0=mv[:, :, 0], scalar=-1.0, in1=rstd[:], op0=ALU.mult,
                                               op1=ALU.mult).then_inc(z_nmr, 1)

            def conv(b, pair):
                for s in range(1, DC):
                    for e in pair:
                        k = ET * b + e
                        if s == 1:
                            dve.wait_ge(tap_now, k + 1)
                        else:
                            dve.wait_ge(tap_past, (DC - 1) * (ET * b + pair[0]) + 2 * (s - 2) + (e - pair[0]) + 1)
                        q = use["conv", b, e]
                        last = nc.vector.scalar_tensor_tensor(
                            out=work[:, e, s:], in0=spare[q % 2][:, :L - s], scalar=taps[:, e, DC - 1 - s:DC - s],
                            in1=work[:, e, s:], op0=ALU.mult, op1=ALU.add).then_inc(tap_past, 1)
                dve.wait_ge(tap_past, (DC - 1) * (ET * b + pair[-1] + 1))
                for e in pair:
                    dve.sem_inc(bank_free[use["conv", b, e] % 2], 1)

            def stage(kind, b, j):
                k = ET * b + j
                if kind == "zstat":
                    z_norm(b)
                elif kind == "conv":
                    conv(b, (j, j + 1))
                elif kind == "zshift":
                    z_shift(b)
                elif kind == "xproj":
                    q = use[kind, b, j]
                    dve.wait_ge(xp_done, b + 1)
                    if b:
                        dve.wait_ge(c_stored, 16 * b)
                        dve.wait_ge(dt_done, ET * b)
                        dve.wait_ge(bt_done, b)
                    nc.vector.tensor_copy(xdbl[:], spare[q % 2][0:R, :]).then_inc(xd_ready, 1)
                    dve.wait_ge(xd_ready, b + 1)
                    dve.sem_inc(bank_free[q % 2], 1)
                elif kind == "dt":
                    q = use[kind, b, j]
                    dve.wait_ge(dt_done, k + 1)
                    if j == 0 and b >= 2:
                        dve.wait_ge(decay_ready, UB * (b - 1))
                    nc.vector.tensor_scalar(delta[:, b % 2, j], spare[q % 2][:], b_dt[:, j:j + 1], None,
                                            ALU.add).then_inc(dt_biased, 1)
                    dve.wait_ge(dt_biased, k + 1)
                    dve.sem_inc(bank_free[q % 2], 1)
                    nc.vector.tensor_scalar(work[:, j], delta[:, b % 2, j], SOFTPLUS_LINEAR, None,
                                            ALU.min).then_inc(dt_capped, 1)
                elif kind == "soft":
                    dve.wait_ge(dt_ln, k + 1)
                    nc.vector.tensor_tensor(delta[:, b % 2, j], delta[:, b % 2, j], work[:, j], ALU.max).then_inc(
                        delta_ready, 1)
                    dve.wait_ge(delta_ready, k + 1)
                    nc.vector.tensor_tensor(work[:, j], delta[:, b % 2, j], u[:, b % 2, j], ALU.mult).then_inc(
                        du_ready, 1)
                elif kind == "skip":
                    dve.wait_ge(summed, UB * (b + 1) - ET + j + 1)
                    nc.vector.scalar_tensor_tensor(out=u[:, b % 2, j], in0=u[:, b % 2, j], scalar=skip[:, j:j + 1],
                                                   in1=acc[j][:], op0=ALU.mult, op1=ALU.add).then_inc(y_skip, 1)
                elif kind == "gate":
                    dve.wait_ge(y_skip, k + 1)
                    dve.wait_ge(zs_ready, ET * (b + 1))
                    nc.vector.tensor_tensor(u[:, b % 2, j], u[:, b % 2, j], zs[:, j], ALU.mult).then_inc(y_gated, 1)
                elif kind == "yt":
                    q = use[kind, b, j]
                    dve.wait_ge(yt_done, k + 1)
                    if k == 0:
                        dve.wait_ge(f_added, ET * (RANK - 1))
                    if b:
                        dve.wait_ge(ht_done, k - TT + 1)
                    nc.vector.tensor_tensor(h[:, j], xin[:, b % 2, j], spare[q % 2][:], ALU.add).then_inc(
                        x1_ready, 1)
                    dve.wait_ge(x1_ready, k + 1)
                    dve.sem_inc(bank_free[q % 2], 1)
                    nc.vector.bn_stats(stats2[:, j], h[:, j]).then_inc(x1_stats, 1)
                    dve.wait_ge(x1_stats, k + 1)
                    if b:
                        dve.wait_ge(x1_ln, k - TT + 1)
                    nc.vector.bn_aggr(mv2[:, j], stats2[:, j]).then_inc(x1_mv, 1)
                elif kind == "norm":
                    dve.wait_ge(x1_rstd, k + 1)
                    dve.wait_ge(x1_biased, k + 1)
                    nc.vector.tensor_scalar(h[:, j], h[:, j], mv2[:, j, 0:1], rstd2[:, j:j + 1],
                                            ALU.subtract, ALU.mult).then_inc(h_ready, 1)
                elif kind == "ffn":
                    q = use[kind, b, j]
                    dve.wait_ge(ffn_done, k + 1)
                    dve.wait_ge(x1_biased, k + 1)
                    nc.vector.scalar_tensor_tensor(out=xin[:, b % 2, j], in0=spare[q % 2][:], scalar=FFN_SCALE,
                                                   in1=xin[:, b % 2, j], op0=ALU.mult, op1=ALU.add).then_inc(
                                                       out_ready, 1)
                    dve.wait_ge(out_ready, k + 1)
                    dve.sem_inc(bank_free[q % 2], 1)

            def unit(b, n, e):
                k = UB * b + ET * n + e
                dve.wait_ge(decay_ready, k + 1)
                dve.wait_ge(dbu_ready, k + 1)
                if k >= SST:
                    dve.wait_ge(multiplied, k - SST + 1)
                nc.vector.tensor_tensor_scan(state[:, e], decay[:, k % SDA], dbu[k % SDBU][:], 0.0, ALU.mult,
                                             ALU.add).then_inc(scanned, 1)

            nc.vector.memset(warm, 0.0).then_inc(warm_set, 1)
            nc.vector.memset(eps[:], LN_EPS).then_inc(eps_set, 1)
            dve.wait_ge(w_small_in, 16 * 2)
            dve.wait_ge(a_exp, 1)
            nc.vector.tensor_scalar(a_neg[:], a_neg[:], -1.0, None, ALU.mult).then_inc(a_ready, 1)
            for b in STEPS:
                for point in range(POINTS):
                    if 0 <= b < NB:
                        for k in (2 * point, 2 * point + 1):
                            unit(b, k // ET, k % ET)
                    for s in stages_at(DVE_POINTS, b, point, NB):
                        stage(*s)

        @block.tensor
        def _(pe):
            def stage(kind, b, j):
                k = ET * b + j
                q = use[kind, b, j]
                bank = spare[q % 2]
                if q >= 2:
                    pe.wait_ge(bank_free[q % 2], q // 2)
                if kind == "conv":
                    if j == 0:
                        pe.wait_ge(ctx_in, 16 * (b + 1))
                    for c in range(KT):
                        last = nc.tensor.matmul(bank[:], w_in[:, c, j * P:(j + 1) * P], ctx_t[:, c], start=(c == 0),
                                                stop=(c == KT - 1))
                    last.then_inc(projected, 1)
                elif kind == "xproj":
                    for e in range(ET):
                        pe.wait_ge(u_ready, ET * b + e + 1)
                        last = nc.tensor.matmul(bank[0:R, :], w_xp[:, e], u[:, b % 2, e], start=(e == 0),
                                                stop=(e == ET - 1))
                    last.then_inc(xp_done, 1)
                elif kind == "bt":
                    pe.wait_ge(xd_ready, b + 1)
                    for t in range(TT):
                        last = nc.tensor.transpose(bank[:, t * R:(t + 1) * R], xdbl[:, t * P:(t + 1) * P],
                                                   ident[0:R, 0:R])
                    last.then_inc(bt_done, 1)
                elif kind == "dt":
                    pe.wait_ge(xd_ready, b + 1)
                    nc.tensor.matmul(bank[:], w_dt[:, j * P:(j + 1) * P], xdbl[0:DR, :], start=True,
                                     stop=True).then_inc(dt_done, 1)
                elif kind == "dut":
                    pe.wait_ge(du_ready, k + 1)
                    for t in range(TT):
                        last = nc.tensor.transpose(bank[:, t * P:(t + 1) * P], work[:, j, t * P:(t + 1) * P], ident[:])
                    last.then_inc(dut_done, 1)
                elif kind == "yt":
                    for e in range(ET):
                        pe.wait_ge(y_gated, ET * b + e + 1)
                        last = nc.tensor.transpose(bank[:, e * P:(e + 1) * P], u[:, b % 2, e, j * P:(j + 1) * P],
                                                   ident[:])
                    last.then_inc(yt_done, 1)
                elif kind == "ht":
                    pe.wait_ge(h_ready, k + 1)
                    for c in range(ET):
                        last = nc.tensor.transpose(bank[:, c * P:(c + 1) * P], h[:, j, c * P:(c + 1) * P],
                                                   ident[:])
                    last.then_inc(ht_done, 1)
                elif kind == "ffn":
                    pe.wait_ge(ht_ready, k + 1)
                    pe.wait_ge(f_added, ET * (RANK - 1))
                    for c in range(ET):
                        last = nc.tensor.matmul(bank[:], h_t[:, j % 2, c], w_ffn[:, c], start=(c == 0),
                                                stop=(c == ET - 1))
                    last.then_inc(ffn_done, 1)

            def unit(b, n, e):
                k = UB * b + ET * n + e
                if e == 0:
                    pe.wait_ge(bx_ready, UB * b + TT * (n + 1))
                if k >= SDBU:
                    pe.wait_ge(scanned, k - SDBU + 1)
                for t in range(TT):
                    last = nc.tensor.transpose(dbu[k % SDBU][:, t * P:(t + 1) * P],
                                               bx_t[:, n % 2, t, e * P:(e + 1) * P], ident[:])
                last.then_inc(dbu_ready, 1)

            def add(b, n, e):
                k = UB * b + ET * n + e
                pe.wait_ge(multiplied, k + 1)
                if n == 0 and b:
                    pe.wait_ge(y_skip, ET * (b - 1) + e + 1)
                nc.tensor.matmul(acc[e][:], ident[:], prod[:, k % SPR], start=(n == 0),
                                 stop=(n == NS - 1)).then_inc(summed, 1)

            pe.wait_ge(warm_set, 1)
            for i in range(WARM):
                nc.tensor.matmul(dbu[0][:], warm[:, 0:P], warm, start=True, stop=True)
            pe.wait_ge(w_proj_in, 16 * 4)
            for b in STEPS:
                if b == NB:
                    for e in range(ET):
                        add(NB - 1, NS - 1, e)
                for point in range(POINTS):
                    if 0 <= b < NB:
                        for k in (2 * point, 2 * point + 1):
                            unit(b, k // ET, k % ET)
                            if k >= ET:
                                add(b, k // ET - 1, k % ET)
                            elif b:
                                add(b - 1, NS - 1, k % ET)
                    for s in stages_at(PE_POINTS, b, point, NB):
                        stage(*s)


_INS = ["x", "ctxT", "winT", "per_channel", "xprojT", "dtprojT", "factors", "ffn_bias", "identity"]


def kernel(x, ctx_1024, L0_xattn_in_proj_w, L0_xattn_conv_w, L0_xattn_conv_b, L0_xattn_x_proj_w, L0_xattn_dt_proj_w,
           L0_xattn_dt_proj_b, L0_xattn_A_log, L0_xattn_D, L0_ffn_factors, L0_ffn_bias):
    import numpy as np
    import concourse.bacc as bacc
    from concourse.bass_utils import run_bass_kernel_spmd

    channels = np.concatenate([L0_xattn_conv_w, np.reshape(L0_xattn_conv_b, (-1, 1)),
                               np.reshape(L0_xattn_dt_proj_b, (-1, 1)), np.reshape(L0_xattn_D, (-1, 1)),
                               L0_xattn_A_log], axis=1)
    arrays = dict(
        x=np.ascontiguousarray(x),
        ctxT=np.ascontiguousarray(np.transpose(ctx_1024, (0, 2, 1))),
        winT=np.ascontiguousarray(np.transpose(L0_xattn_in_proj_w)),
        per_channel=np.ascontiguousarray(channels.reshape(-1, P, channels.shape[1]).transpose(1, 0, 2)),
        xprojT=np.ascontiguousarray(np.transpose(L0_xattn_x_proj_w)),
        dtprojT=np.ascontiguousarray(np.transpose(L0_xattn_dt_proj_w)),
        factors=np.ascontiguousarray(L0_ffn_factors),
        ffn_bias=np.ascontiguousarray(L0_ffn_bias),
        identity=np.eye(P, dtype=np.float32),
    )
    nc = bacc.Bacc("TRN2", target_bir_lowering=False, num_devices=1)
    args = [nc.dram_tensor(n, arrays[n].shape, mybir.dt.from_np(arrays[n].dtype), kind="ExternalInput").ap()
            for n in _INS]
    out = nc.dram_tensor("out", x.shape, F32, kind="ExternalOutput").ap()
    ssm_ffn_kernel(nc, *args, out)
    r = run_bass_kernel_spmd(nc, [arrays], core_ids=[0])
    return r.results[0]["out"]
```

```python
from contextlib import ExitStack

import concourse.bass as bass
from concourse import mybir

ALU = mybir.AluOpType
ACT = mybir.ActivationFunctionType
F32 = mybir.dt.float32

P = 128
LN_EXP = "natural_log_exp_and_others"
LN_EPS = 1e-5
SOFTPLUS_LINEAR = 30.0


NEXT, OWN, LAST = 1, 0, -1
OFFSET = dict(conv=NEXT, usilu=NEXT, xproj0=NEXT, xproj=NEXT, bt=NEXT, dt=NEXT, soft=NEXT, dut=NEXT,
              zstat=OWN, zrstd=OWN, znorm=OWN, zt=OWN, gatesilu=OWN,
              gate=LAST, x1=LAST, rstd=LAST, norm=LAST, bias=LAST, ht=LAST, ffn0=LAST, ffn=LAST)
PE_POINTS = {1: [("conv", 0), ("conv", 1)], 3: [("conv", 2)], 8: [("conv", 3)], 11: [("zt", 0), ("zt", 1)],
             12: [("zt", 2)], 13: [("ht", 0), ("zt", 3)], 14: [("ht", 1), ("ffn0", 0), ("ffn", 0)],
             15: [("xproj0", 0), ("ffn0", 1)], 16: [("xproj", 0)], 17: [("ffn", 1), ("bt", 0)],
             18: [("dt", 0), ("ht", 2)], 19: [("dt", 1), ("dt", 2)], 20: [("ht", 3)], 21: [("dt", 3), ("ffn0", 2)],
             24: [("ffn", 2)], 25: [("ffn0", 3)], 27: [("ffn", 3)], 28: [("dut", 0)],
             29: [("dut", 1), ("dut", 2), ("dut", 3)]}
ACT_POINTS = {3: [("conv", 0), ("conv", 1)], 7: [("conv", 2)], 11: [("conv", 3)], 13: [("rstd", 0), ("zrstd", 0)],
              14: [("rstd", 1), ("gatesilu", 0), ("gatesilu", 1), ("usilu", 0), ("gatesilu", 2), ("ht", 0),
                   ("gatesilu", 3), ("ht", 1), ("rstd", 2)],
              17: [("rstd", 3)], 20: [("bt", 0)], 21: [("ht", 2)], 23: [("dt", 0), ("ht", 3), ("dt", 1)],
              26: [("dt", 2)], 27: [("dt", 3)], 31: [("dut", 0), ("dut", 1), ("dut", 2), ("dut", 3)]}
DVE_POINTS = {1: [("gate", 0), ("gate", 1), ("gate", 2), ("gate", 3), ("zstat", 0)], 2: [("conv", 0)], 7: [("x1", 0)],
              8: [("x1", 1)], 10: [("conv", 2)],
              11: [("znorm", 0), ("znorm", 1), ("znorm", 2), ("norm", 0), ("znorm", 3), ("norm", 1)], 13: [("x1", 2)],
              14: [("x1", 3), ("ffn", 0)], 16: [("norm", 2), ("xproj", 0)], 17: [("norm", 3), ("ffn", 1)],
              18: [("dt", 0)], 19: [("dt", 1)], 20: [("dt", 2)], 21: [("dt", 3)], 23: [("soft", 0)],
              25: [("soft", 1), ("ffn", 2)], 26: [("soft", 2)], 27: [("ffn", 3)], 28: [("soft", 3)]}
POOL_POINTS = {9: [("bias", 0)], 10: [("bias", 1)], 13: [("bias", 2)], 14: [("bias", 3)]}


LATE_EVERY = 2
DVE_TILES = 1


CLAIMED_BY = dict(gatesilu="zt", xproj="xproj0", ffn="ffn0")


def in_acc(kind, b, j, batches):
    return (b == 0 and kind in ("conv", "dt", "dut")) or (b == batches - 1 and kind in ("ffn0", "ffn"))


def stages_at(points, step, point, batches):
    return [(kind, step + OFFSET[kind], j) for kind, j in points.get(point, ()) if 0 <= step + OFFSET[kind] < batches]


def ssm_ffn_kernel(nc, x, ctxT, winT, per_channel, xprojT, dtprojT, factors, ffn_bias, identity, out):
    NB, L, DI = x.shape
    DM = ctxT.shape[1]
    R = xprojT.shape[1]
    DR = dtprojT.shape[0]
    NS = (R - DR) // 2
    DC = per_channel.shape[2] - NS - 3
    RANK = factors.shape[0]
    ET = DI // P
    TT = L // P
    KT = DM // P
    FFN_SCALE = float(RANK) ** -0.5
    assert L == DI == 512 and NS % 4 == 0 and ET == TT == 4

    UB = NS * ET
    POINTS = UB // 2
    GROUPS = 4
    NG = NS // GROUPS
    SDBU = 2
    SDA = 2 * ET
    SST = ET
    SPR = 2 * ET
    WARM = 5
    F_EARLY = 5
    LAG = ET
    STEPS = range(-1, NB + 1)
    use = {}
    for b in STEPS:
        for point in range(POINTS):
            for s in stages_at(PE_POINTS, b, point, NB):
                if s[0] not in CLAIMED_BY and not in_acc(*s, NB):
                    use[s] = len(use)

    def late_tiles(n):
        return DVE_TILES if n % LATE_EVERY == LATE_EVERY - 1 else 0

    def late_until(rows):
        return rows // LATE_EVERY * DVE_TILES

    def unit_of(k):
        return k // UB, k % UB // ET, k % ET

    with ExitStack() as ctx:
        def sb(name, shape):
            return ctx.enter_context(nc.sbuf_tensor(name, shape, F32))

        def sem(name):
            return ctx.enter_context(nc.semaphore(name))

        ident = sb("ident", [P, P])
        w_in = sb("w_in", [P, KT, DI])
        w_xp = sb("w_xp", [P, ET, R])
        w_dt = sb("w_dt", [DR, DI])
        chan = sb("chan", [P, ET, DC + 3 + NS])
        taps = chan[:, :, 0:DC]
        b_conv, b_dt, d_skip = (chan[:, :, DC + i] for i in range(3))
        a_log = chan[:, :, DC + 3:]
        a_neg = sb("a_neg", [P, ET, NS])
        bias_row = sb("bias_row", [P, DI])
        eps = sb("eps", [P, 1])
        d_diag = sb("d_diag", [P, ET, P])
        w_ffn = sb("w_ffn", [P, ET, DI])
        xin = sb("xin", [P, 2, ET, L])
        u = sb("u", [P, ET, L])
        delta = sb("delta", [P, 2, ET, L])
        work = sb("work", [P, ET, L])
        ctx_t = sb("ctx_t", [P, KT, L])
        zs = sb("zs", [P, ET, L])
        xdbl = sb("xdbl", [R, L])
        bt = sb("bt", [P, 2, TT, R])
        du_t = sb("du_t", [P, 2, TT, DI])
        c_row = sb("c_row", [P, NS, L])
        stats = sb("stats", [P, ET, 6])
        mv = sb("mv", [P, ET, 2])
        rstd = sb("rstd", [P, ET])
        lnv = sb("lnv", [P, ET])
        bx_t = sb("bx_t", [P, 2, TT, DI])
        decay = sb("decay", [P, SDA, L])
        state = sb("state", [P, SST, L])
        prod = sb("prod", [P, SPR, L])
        h = sb("h", [P, TT, DI])
        h_t = sb("h_t", [P, 2, ET, P])
        stats2 = sb("stats2", [P, TT, 6])
        mv2 = sb("mv2", [P, TT, 2])
        lnv2 = sb("lnv2", [P, TT])
        rstd2 = sb("rstd2", [P, TT])

        warm = state[:, 0]

        dbu = [ctx.enter_context(nc.psum_tensor(f"dbu{i}", [P, L], F32)) for i in range(SDBU)]
        acc = [ctx.enter_context(nc.psum_tensor(f"acc{i}", [P, L], F32)) for i in range(ET)]
        spare = [ctx.enter_context(nc.psum_tensor(f"spare{i}", [P, L], F32)) for i in range(2)]

        def bank_of(kind, b, j):
            kind = CLAIMED_BY.get(kind, kind)
            return acc[j] if in_acc(kind, b, j, NB) else spare[use[kind, b, j] % 2]

        def release(eng, kind, b, j):
            kind = CLAIMED_BY.get(kind, kind)
            if not in_acc(kind, b, j, NB):
                eng.sem_inc(bank_free[use[kind, b, j] % 2], 1)

        def taps_until(b, s, e):
            if b == 0:
                return (s - 1) * ET + e + 1
            return (DC - 1) * (ET * b + e // 2 * 2) + (s - 1) * 2 + e % 2 + 1

        c_dram = nc.dram_tensor("c_scratch", [NB, NS, L], F32, kind="Internal").ap()

        w_proj_in = sem("w_proj_in")
        w_small_in = sem("w_small_in")
        ctx_in = sem("ctx_in")
        x_in = sem("x_in")
        f_in = [sem(f"f_in{i}") for i in range(2)]
        c_stored = sem("c_stored")
        c_in = [sem(f"c_in{i}") for i in range(GROUPS)]
        stored = sem("stored")
        f_added = sem("f_added")
        warm_set = sem("warm_set")
        eps_set = sem("eps_set")
        a_exp = sem("a_exp")
        a_ready = sem("a_ready")
        d_ready = sem("d_ready")
        projected = sem("projected")
        tap_now = sem("tap_now")
        tap_past = sem("tap_past")
        u_ready = sem("u_ready")
        z_stats = sem("z_stats")
        z_mv = sem("z_mv")
        z_ln = sem("z_ln")
        z_rstd = sem("z_rstd")
        z_normed = sem("z_normed")
        zt_done = sem("zt_done")
        zs_ready = sem("zs_ready")
        xp_done = sem("xp_done")
        xd_ready = sem("xd_ready")
        bt_done = sem("bt_done")
        bt_ready = sem("bt_ready")
        dt_done = sem("dt_done")
        dt_biased = sem("dt_biased")
        dt_capped = sem("dt_capped")
        dt_exp = sem("dt_exp")
        dt_ln = sem("dt_ln")
        delta_ready = sem("delta_ready")
        du_ready = sem("du_ready")
        dut_done = sem("dut_done")
        dut_ready = sem("dut_ready")
        bank_free = [sem(f"bank_free{i}") for i in range(2)]
        bx_ready = sem("bx_ready")
        bx_late_ready = sem("bx_late_ready")
        decay_ready = sem("decay_ready")
        dbu_ready = sem("dbu_ready")
        scanned = sem("scanned")
        multiplied = sem("multiplied")
        u_used = sem("u_used")
        summed = sem("summed")
        y_gated = sem("y_gated")
        x1_ready = sem("x1_ready")
        x1_stats = sem("x1_stats")
        x1_mv = sem("x1_mv")
        x1_ln = sem("x1_ln")
        x1_rstd = sem("x1_rstd")
        x1_biased = sem("x1_biased")
        h_ready = sem("h_ready")
        ht_done = sem("ht_done")
        ht_ready = sem("ht_ready")
        ffn_done = sem("ffn_done")
        out_ready = sem("out_ready")

        block = ctx.enter_context(nc.Block())

        @block.sync
        def _(sp):
            sp.dma_start(w_in[:], winT.rearrange("(k p) e -> p k e", p=P)).then_inc(w_proj_in, 16)
            sp.dma_start(ctx_t[:], ctxT[0].rearrange("(k p) t -> p k t", p=P)).then_inc(ctx_in, 16)
            sp.dma_start(chan[:], per_channel).then_inc(w_small_in, 16)
            sp.dma_start(xin[:, 0], x[0].rearrange("(k p) t -> p k t", p=P)).then_inc(x_in, 16)
            sp.dma_start(ident[:], identity).then_inc(w_proj_in, 16)
            sp.dma_start(w_xp[:], xprojT.rearrange("(k p) r -> p k r", p=P)).then_inc(w_proj_in, 16)
            sp.dma_start(w_dt[:], dtprojT).then_inc(w_proj_in, 16)
            sp.dma_start(bias_row[:], ffn_bias.rearrange("(o e) -> o e", o=1).broadcast_to([P, DI])).then_inc(
                w_small_in, 16)
            sp.dma_start(xin[:, 1], x[1].rearrange("(k p) t -> p k t", p=P)).then_inc(x_in, 16)

            def load_factor(r):
                if r >= 2:
                    sp.wait_ge(f_added, max(ET * (r - 2), ET))
                sp.dma_start((zs, h)[r % 2][:], factors[r].rearrange("(k p) e -> p k e", p=P)).then_inc(f_in[r % 2], 16)

            for r in range(F_EARLY):
                load_factor(r)

            def load_c(b):
                sp.wait_ge(xd_ready, b + 1)
                sp.dma_start(c_dram[b], xdbl[DR + NS:R, :]).then_inc(c_stored, 16)
                sp.wait_ge(c_stored, 16 * (b + 1))
                for g in range(GROUPS):
                    rows = slice(NG * g, NG * (g + 1))
                    if b:
                        sp.wait_ge(multiplied, UB * (b - 1) + ET * NG * (g + 1))
                    sp.dma_start(c_row[:, rows], c_dram[b:b + 1, rows].broadcast_to([P, NG, L])).then_inc(c_in[g], 16)

            def load_x(b):
                if b >= 2:
                    sp.wait_ge(stored, 16 * TT * (b - 1))
                sp.dma_start(xin[:, b % 2], x[b].rearrange("(k p) t -> p k t", p=P)).then_inc(x_in, 16)

            def store_out(b, tiles):
                for j in tiles:
                    sp.wait_ge(out_ready, TT * b + j + 1)
                    sp.dma_start(out[b, j * P:(j + 1) * P, :], xin[:, b % 2, j]).then_inc(stored, 16)

            def load_context(b):
                sp.wait_ge(projected, ET * b)
                sp.dma_start(ctx_t[:], ctxT[b].rearrange("(k p) t -> p k t", p=P)).then_inc(ctx_in, 16)

            load_context(1)
            load_c(0)
            for r in range(F_EARLY, RANK):
                load_factor(r)
            for b in range(NB):
                if b:
                    store_out(b - 1, range(TT))
                    if b + 1 < NB:
                        load_x(b + 1)
                if b + 2 < NB:
                    load_context(b + 2)
                if b + 1 < NB:
                    load_c(b + 1)
            store_out(NB - 1, range(TT))
            sp.wait_ge(stored, 16 * TT * NB)

        @block.gpsimd
        def _(pool):
            def add_factor(r, j):
                if r == 1:
                    pool.wait_ge(f_in[0], 16)
                else:
                    pool.wait_ge(f_added, ET * (r - 2) + j + 1)
                pool.wait_ge(f_in[r % 2], 16 * (r // 2 + 1))
                nc.gpsimd.tensor_tensor(w_ffn[:, j], zs[:, j] if r == 1 else w_ffn[:, j], (zs, h)[r % 2][:, j],
                                        ALU.add).then_inc(f_added, 1)

            def unit(b, n, e):
                k = UB * b + ET * n + e
                if e == 0 and n % NG == 0:
                    pool.wait_ge(c_in[n // NG], 16 * (b + 1))
                pool.wait_ge(scanned, k + 1)
                if k >= SPR:
                    pool.wait_ge(summed, k - SPR + 1)
                nc.gpsimd.tensor_tensor(prod[:, k % SPR], state[:, k % SST], c_row[:, n], ALU.mult).then_inc(
                    multiplied, 1)

            def stage(kind, b, j):
                if kind == "bias":
                    pool.wait_ge(x1_ready, TT * b + j + 1)
                    nc.gpsimd.tensor_tensor(xin[:, b % 2, j], h[:, j], bias_row[:], ALU.add).then_inc(x1_biased, 1)

            for b in STEPS:
                for point in range(POINTS):
                    if 0 <= b < NB:
                        for k in (2 * point, 2 * point + 1):
                            unit(b, k // ET, k % ET)
                        if b == 0 and ET * (F_EARLY - 1) + point < ET * (RANK - 1):
                            k = ET * (F_EARLY - 1) + point
                            add_factor(k // ET + 1, k % ET)
                    for s in stages_at(POOL_POINTS, b, point, NB):
                        stage(*s)
                if b < 0:
                    for r in range(1, F_EARLY):
                        for j in range(ET):
                            add_factor(r, j)

        @block.scalar
        def _(act):
            def copy_conv(b, e):
                k = ET * b + e
                act.wait_ge(projected, k + 1)
                if e == 0 and b:
                    act.wait_ge(dut_done, ET * b)
                nc.scalar.activation(work[:, e], bank_of("conv", b, e)[:], ACT.Copy,
                                     scale=taps[:, e, DC - 1:DC]).then_inc(tap_now, 1)

            def stage(kind, b, j):
                k = ET * b + j
                if kind == "conv":
                    copy_conv(b, j)
                elif kind == "zrstd":
                    act.wait_ge(z_mv, ET * (b + 1))
                    nc.scalar.activation(lnv[:], mv[:, :, 1], ACT.Ln, bias=eps[:, 0:1]).then_inc(z_ln, 1)
                    act.wait_ge(z_ln, b + 1)
                    nc.scalar.activation(rstd[:], lnv[:], ACT.Exp, scale=-0.5).then_inc(z_rstd, 1)
                elif kind == "usilu":
                    for e in range(ET):
                        act.wait_ge(tap_past, taps_until(b, DC - 1, e))
                        if b:
                            act.wait_ge(u_used, ET * (b - 1) + e + 1)
                        nc.scalar.activation(u[:, e], work[:, e], ACT.Silu, bias=b_conv[:, e:e + 1]).then_inc(
                            u_ready, 1)
                    if b == 0:
                        nc.scalar.preload_act_table_set(LN_EXP)
                elif kind == "gatesilu":
                    act.wait_ge(zt_done, k + 1)
                    nc.scalar.activation(zs[:, j], bank_of(kind, b, j)[:], ACT.Silu).then_inc(zs_ready, 1)
                    act.wait_ge(zs_ready, k + 1)
                    release(act, kind, b, j)
                    if j == ET - 1:
                        nc.scalar.preload_act_table_set(LN_EXP)
                elif kind == "bt":
                    act.wait_ge(bt_done, b + 1)
                    nc.scalar.copy(bt[:, b % 2], bank_of(kind, b, j)[:, 0:TT * R].rearrange("p (j r) -> p j r", r=R)
                                   ).then_inc(bt_ready, 1)
                    act.wait_ge(bt_ready, b + 1)
                    release(act, kind, b, j)
                elif kind == "dt":
                    act.wait_ge(dt_capped, k + 1)
                    nc.scalar.activation(work[:, j], work[:, j], ACT.Exp).then_inc(dt_exp, 1)
                    act.wait_ge(dt_exp, k + 1)
                    nc.scalar.activation(work[:, j], work[:, j], ACT.Ln, bias=1.0).then_inc(dt_ln, 1)
                elif kind == "dut":
                    act.wait_ge(dut_done, k + 1)
                    nc.scalar.copy(du_t[:, b % 2, :, j * P:(j + 1) * P],
                                   bank_of(kind, b, j)[:].rearrange("p (j c) -> p j c", c=P)).then_inc(dut_ready, 1)
                    act.wait_ge(dut_ready, k + 1)
                    release(act, kind, b, j)
                elif kind == "rstd":
                    act.wait_ge(x1_mv, k + 1)
                    nc.scalar.activation(lnv2[:, j:j + 1], mv2[:, j, 1:2], ACT.Ln, bias=eps[:, 0:1]
                                         ).then_inc(x1_ln, 1)
                    act.wait_ge(x1_ln, k + 1)
                    if b:
                        act.wait_ge(h_ready, k - TT + 1)
                    nc.scalar.activation(rstd2[:, j:j + 1], lnv2[:, j:j + 1], ACT.Exp, scale=-0.5
                                         ).then_inc(x1_rstd, 1)
                elif kind == "ht":
                    act.wait_ge(ht_done, k + 1)
                    if k >= 2:
                        act.wait_ge(ffn_done, k - 1)
                    nc.scalar.copy(h_t[:, j % 2], bank_of(kind, b, j)[:].rearrange("p (k t) -> p k t", t=P)).then_inc(
                        ht_ready, 1)
                    act.wait_ge(ht_ready, k + 1)
                    release(act, kind, b, j)

            def unit(b, n, e):
                k = UB * b + ET * n + e
                if e == 0:
                    if UB * b + ET * n >= 2 * ET:
                        act.wait_ge(dbu_ready, UB * b + ET * (n - 1))
                    for j in range(TT - late_tiles(n)):
                        nc.scalar.activation(bx_t[:, n % 2, j], du_t[:, b % 2, j], ACT.Copy,
                                             scale=bt[:, b % 2, j, DR + n:DR + n + 1]).then_inc(bx_ready, 1)
                if k >= SDA:
                    act.wait_ge(scanned, k - SDA + 1)
                nc.scalar.activation(decay[:, k % SDA], delta[:, b % 2, e], ACT.Exp,
                                     scale=a_neg[:, e, n:n + 1]).then_inc(decay_ready, 1)

            nc.scalar.preload_act_table_set(LN_EXP)
            act.wait_ge(w_small_in, 16 * 2)
            nc.scalar.activation(a_neg[:], a_log, ACT.Exp).then_inc(a_exp, 1)
            act.wait_ge(eps_set, 1)
            for b in STEPS:
                if 0 <= b < NB:
                    act.wait_ge(a_ready, 1)
                    act.wait_ge(delta_ready, ET * (b + 1))
                    act.wait_ge(dut_ready, ET * (b + 1))
                    act.wait_ge(bt_ready, b + 1)
                for point in range(POINTS):
                    if 0 <= b < NB:
                        for k in (2 * point, 2 * point + 1):
                            unit(b, k // ET, k % ET)
                    for s in stages_at(ACT_POINTS, b, point, NB):
                        stage(*s)

        @block.vector
        def _(dve):
            def z_norm(b):
                dve.wait_ge(x_in, 16 * (b + 1))
                if b:
                    dve.wait_ge(z_normed, ET * b)
                for e in range(ET):
                    nc.vector.bn_stats(stats[:, e], xin[:, b % 2, e]).then_inc(z_stats, 1)
                for e in range(ET):
                    dve.wait_ge(z_stats, ET * b + e + 1)
                    nc.vector.bn_aggr(mv[:, e], stats[:, e]).then_inc(z_mv, 1)

            def conv(b, tiles):
                for s in range(1, DC):
                    for e in tiles:
                        if s == 1:
                            dve.wait_ge(tap_now, ET * b + e + 1)
                        else:
                            dve.wait_ge(tap_past, taps_until(b, s - 1, e))
                        nc.vector.scalar_tensor_tensor(
                            out=work[:, e, s:], in0=bank_of("conv", b, e)[:, :L - s],
                            scalar=taps[:, e, DC - 1 - s:DC - s], in1=work[:, e, s:], op0=ALU.mult,
                            op1=ALU.add).then_inc(tap_past, 1)
                dve.wait_ge(tap_past, taps_until(b, DC - 1, tiles[-1]))
                for e in tiles:
                    release(dve, "conv", b, e)

            def scale_late(b, n):
                row = NS * b + n
                if row >= 2 and late_tiles(n):
                    dve.wait_ge(dbu_ready, ET * (row - 1))
                for j in range(TT - late_tiles(n), TT):
                    nc.vector.tensor_scalar(bx_t[:, n % 2, j], du_t[:, b % 2, j], bt[:, b % 2, j, DR + n:DR + n + 1],
                                            None, ALU.mult).then_inc(bx_late_ready, 1)

            def stage(kind, b, j):
                k = ET * b + j
                if kind == "zstat":
                    z_norm(b)
                elif kind == "conv":
                    if b:
                        conv(b, (j, j + 1))
                    elif j == 0:
                        conv(b, range(ET))
                elif kind == "znorm":
                    dve.wait_ge(z_rstd, b + 1)
                    dve.wait_ge(z_mv, ET * (b + 1))
                    if b:
                        dve.wait_ge(y_gated, TT * b)
                    else:
                        dve.wait_ge(f_added, ET * (RANK - 1))
                    nc.vector.tensor_scalar(zs[:, j], xin[:, b % 2, j], mv[:, j, 0:1], rstd[:, j:j + 1],
                                            ALU.subtract, ALU.mult).then_inc(z_normed, 1)
                elif kind == "xproj":
                    dve.wait_ge(xp_done, b + 1)
                    if b:
                        dve.wait_ge(c_stored, 16 * b)
                        dve.wait_ge(dt_done, ET * b)
                        dve.wait_ge(bt_done, b)
                    nc.vector.tensor_copy(xdbl[:], bank_of(kind, b, j)[0:R, :]).then_inc(xd_ready, 1)
                    dve.wait_ge(xd_ready, b + 1)
                    release(dve, kind, b, j)
                elif kind == "dt":
                    dve.wait_ge(dt_done, k + 1)
                    if j == 0 and b >= 2:
                        dve.wait_ge(decay_ready, UB * (b - 1))
                    nc.vector.tensor_scalar(delta[:, b % 2, j], bank_of(kind, b, j)[:], b_dt[:, j:j + 1], None,
                                            ALU.add).then_inc(dt_biased, 1)
                    dve.wait_ge(dt_biased, k + 1)
                    release(dve, kind, b, j)
                    nc.vector.tensor_scalar(work[:, j], delta[:, b % 2, j], SOFTPLUS_LINEAR, None,
                                            ALU.min).then_inc(dt_capped, 1)
                elif kind == "soft":
                    dve.wait_ge(dt_ln, k + 1)
                    nc.vector.tensor_tensor(delta[:, b % 2, j], delta[:, b % 2, j], work[:, j], ALU.max).then_inc(
                        delta_ready, 1)
                    dve.wait_ge(delta_ready, k + 1)
                    nc.vector.tensor_tensor(work[:, j], delta[:, b % 2, j], u[:, j], ALU.mult).then_inc(
                        du_ready, 1)
                elif kind == "gate":
                    dve.wait_ge(summed, UB * (b + 1))
                    dve.wait_ge(zs_ready, ET * (b + 1))
                    if k == 0:
                        dve.wait_ge(f_added, ET * (RANK - 1))
                    if b:
                        dve.wait_ge(ht_done, k - TT + 1)
                    nc.vector.tensor_tensor(h[:, j].rearrange("p (e c) -> p e c", c=P),
                                            acc[j][:].rearrange("p (e c) -> p e c", c=P),
                                            zs[:, :, j * P:(j + 1) * P], ALU.mult).then_inc(y_gated, 1)
                elif kind == "x1":
                    dve.wait_ge(y_gated, k + 1)
                    nc.vector.tensor_tensor(h[:, j], h[:, j], xin[:, b % 2, j], ALU.add).then_inc(x1_ready, 1)
                    dve.wait_ge(x1_ready, k + 1)
                    nc.vector.bn_stats(stats2[:, j], h[:, j]).then_inc(x1_stats, 1)
                    dve.wait_ge(x1_stats, k + 1)
                    if b:
                        dve.wait_ge(x1_ln, k - TT + 1)
                    nc.vector.bn_aggr(mv2[:, j], stats2[:, j]).then_inc(x1_mv, 1)
                elif kind == "norm":
                    dve.wait_ge(x1_rstd, k + 1)
                    dve.wait_ge(x1_biased, k + 1)
                    nc.vector.tensor_scalar(h[:, j], h[:, j], mv2[:, j, 0:1], rstd2[:, j:j + 1],
                                            ALU.subtract, ALU.mult).then_inc(h_ready, 1)
                elif kind == "ffn":
                    dve.wait_ge(ffn_done, k + 1)
                    dve.wait_ge(x1_biased, k + 1)
                    nc.vector.scalar_tensor_tensor(out=xin[:, b % 2, j], in0=bank_of(kind, b, j)[:], scalar=FFN_SCALE,
                                                   in1=xin[:, b % 2, j], op0=ALU.mult, op1=ALU.add).then_inc(
                                                       out_ready, 1)
                    dve.wait_ge(out_ready, k + 1)
                    release(dve, kind, b, j)

            def unit(b, n, e):
                k = UB * b + ET * n + e
                if k % UB == 0:
                    dve.wait_ge(dut_ready, ET * (b + 1))
                    dve.wait_ge(bt_ready, b + 1)
                    scale_late(b, 0)
                if e == 0 and n + 1 < NS:
                    scale_late(b, n + 1)
                dve.wait_ge(decay_ready, k + 1)
                dve.wait_ge(dbu_ready, k + 1)
                if k >= SST:
                    dve.wait_ge(multiplied, k - SST + 1)
                nc.vector.tensor_tensor_scan(state[:, k % SST], decay[:, k % SDA], dbu[k % SDBU][:], 0.0, ALU.mult,
                                             ALU.add).then_inc(scanned, 1)

            nc.vector.memset(warm, 0.0).then_inc(warm_set, 1)
            nc.vector.memset(eps[:], LN_EPS).then_inc(eps_set, 1)
            dve.wait_ge(w_small_in, 16 * 2)
            dve.wait_ge(a_exp, 1)
            nc.vector.tensor_scalar(a_neg[:], a_neg[:], -1.0, None, ALU.mult).then_inc(a_ready, 1)
            dve.wait_ge(w_proj_in, 16 * 4)
            for e in range(ET):
                nc.vector.tensor_scalar(d_diag[:, e], ident[:], d_skip[:, e:e + 1], None, ALU.mult).then_inc(
                    d_ready, 1)
            for b in STEPS:
                for point in range(POINTS):
                    if 0 <= b < NB:
                        for k in (2 * point, 2 * point + 1):
                            unit(b, k // ET, k % ET)
                    for s in stages_at(DVE_POINTS, b, point, NB):
                        stage(*s)

        @block.tensor
        def _(pe):
            def stage(kind, b, j):
                k = ET * b + j
                bank = bank_of(kind, b, j)
                if kind in CLAIMED_BY:
                    pass
                elif not in_acc(kind, b, j, NB) and use[kind, b, j] >= 2:
                    pe.wait_ge(bank_free[use[kind, b, j] % 2], use[kind, b, j] // 2)
                elif kind == "dt" and b == 0:
                    pe.wait_ge(tap_past, taps_until(b, DC - 1, j))
                elif kind == "dut" and b == 0:
                    pe.wait_ge(dt_biased, j + 1)
                elif kind == "ffn0" and b == NB - 1:
                    pe.wait_ge(y_gated, k + 1)
                if kind == "conv":
                    if j == 0:
                        pe.wait_ge(ctx_in, 16 * (b + 1))
                    for c in range(KT):
                        last = nc.tensor.matmul(bank[:], w_in[:, c, j * P:(j + 1) * P], ctx_t[:, c], start=(c == 0),
                                                stop=(c == KT - 1))
                    last.then_inc(projected, 1)
                elif kind in ("xproj0", "xproj"):
                    for e in range(2) if kind == "xproj0" else range(2, ET):
                        pe.wait_ge(u_ready, ET * b + e + 1)
                        last = nc.tensor.matmul(bank[0:R, :], w_xp[:, e], u[:, e], start=(e == 0),
                                                stop=(e == ET - 1))
                    if kind == "xproj":
                        last.then_inc(xp_done, 1)
                elif kind == "bt":
                    pe.wait_ge(xd_ready, b + 1)
                    for t in range(TT):
                        last = nc.tensor.transpose(bank[:, t * R:(t + 1) * R], xdbl[:, t * P:(t + 1) * P],
                                                   ident[0:R, 0:R])
                    last.then_inc(bt_done, 1)
                elif kind == "dt":
                    pe.wait_ge(xd_ready, b + 1)
                    nc.tensor.matmul(bank[:], w_dt[:, j * P:(j + 1) * P], xdbl[0:DR, :], start=True,
                                     stop=True).then_inc(dt_done, 1)
                elif kind == "dut":
                    pe.wait_ge(du_ready, k + 1)
                    for t in range(TT):
                        last = nc.tensor.transpose(bank[:, t * P:(t + 1) * P], work[:, j, t * P:(t + 1) * P], ident[:])
                    last.then_inc(dut_done, 1)
                elif kind == "zt":
                    pe.wait_ge(z_normed, k + 1)
                    for t in range(TT):
                        last = nc.tensor.transpose(bank[:, t * P:(t + 1) * P], zs[:, j, t * P:(t + 1) * P], ident[:])
                    last.then_inc(zt_done, 1)
                elif kind == "ht":
                    pe.wait_ge(h_ready, k + 1)
                    for c in range(ET):
                        last = nc.tensor.transpose(bank[:, c * P:(c + 1) * P], h[:, j, c * P:(c + 1) * P],
                                                   ident[:])
                    last.then_inc(ht_done, 1)
                elif kind in ("ffn0", "ffn"):
                    pe.wait_ge(ht_ready, k + 1)
                    pe.wait_ge(f_added, ET * (RANK - 1))
                    for c in range(2) if kind == "ffn0" else range(2, ET):
                        last = nc.tensor.matmul(bank[:], h_t[:, j % 2, c], w_ffn[:, c], start=(c == 0),
                                                stop=(c == ET - 1))
                    if kind == "ffn":
                        last.then_inc(ffn_done, 1)

            def unit(b, n, e):
                k = UB * b + ET * n + e
                if e == 0:
                    pe.wait_ge(bx_ready, TT * (NS * b + n + 1) - late_until(NS * b + n + 1))
                    if late_until(NS * b + n + 1):
                        pe.wait_ge(bx_late_ready, late_until(NS * b + n + 1))
                if k >= SDBU:
                    pe.wait_ge(scanned, k - SDBU + 1)
                for t in range(TT):
                    last = nc.tensor.transpose(dbu[k % SDBU][:, t * P:(t + 1) * P],
                                               bx_t[:, n % 2, t, e * P:(e + 1) * P], ident[:])
                last.then_inc(dbu_ready, 1)

            def start_sums(b, e):
                if b == 0 and e == 0:
                    pe.wait_ge(d_ready, ET)
                for j in range(TT):
                    if b and e == 0:
                        pe.wait_ge(y_gated, TT * (b - 1) + j + 1)
                    last = nc.tensor.matmul(acc[j][:, e * P:(e + 1) * P], u[:, e, j * P:(j + 1) * P], d_diag[:, e],
                                            start=(e == 0), stop=False, skip_group_check=True)
                last.then_inc(u_used, 1)

            def add(b, n, e):
                if n == 0:
                    start_sums(b, e)
                k = UB * b + ET * n + e
                pe.wait_ge(multiplied, k + 1)
                for j in range(TT):
                    last = nc.tensor.matmul(acc[j][:, e * P:(e + 1) * P], prod[:, k % SPR, j * P:(j + 1) * P],
                                            ident[:], start=False, stop=(n == NS - 1), is_transpose=True,
                                            skip_group_check=True)
                last.then_inc(summed, 1)

            pe.wait_ge(warm_set, 1)
            for i in range(WARM):
                nc.tensor.matmul(dbu[0][:], warm[:, 0:P], warm, start=True, stop=True)
            pe.wait_ge(w_proj_in, 16 * 4)
            for b in STEPS:
                if b == NB:
                    for k in range(NB * UB - LAG, NB * UB):
                        add(*unit_of(k))
                for point in range(POINTS):
                    if 0 <= b < NB:
                        for k in (2 * point, 2 * point + 1):
                            unit(b, k // ET, k % ET)
                            if UB * b + k >= LAG:
                                add(*unit_of(UB * b + k - LAG))
                    for s in stages_at(PE_POINTS, b, point, NB):
                        stage(*s)


_INS = ["x", "ctxT", "winT", "per_channel", "xprojT", "dtprojT", "factors", "ffn_bias", "identity"]


def kernel(x, ctx_1024, L0_xattn_in_proj_w, L0_xattn_conv_w, L0_xattn_conv_b, L0_xattn_x_proj_w, L0_xattn_dt_proj_w,
           L0_xattn_dt_proj_b, L0_xattn_A_log, L0_xattn_D, L0_ffn_factors, L0_ffn_bias):
    import numpy as np
    import concourse.bacc as bacc
    from concourse.bass_utils import run_bass_kernel_spmd

    channels = np.concatenate([L0_xattn_conv_w, np.reshape(L0_xattn_conv_b, (-1, 1)),
                               np.reshape(L0_xattn_dt_proj_b, (-1, 1)), np.reshape(L0_xattn_D, (-1, 1)),
                               L0_xattn_A_log], axis=1)
    arrays = dict(
        x=np.ascontiguousarray(x),
        ctxT=np.ascontiguousarray(np.transpose(ctx_1024, (0, 2, 1))),
        winT=np.ascontiguousarray(np.transpose(L0_xattn_in_proj_w)),
        per_channel=np.ascontiguousarray(channels.reshape(-1, P, channels.shape[1]).transpose(1, 0, 2)),
        xprojT=np.ascontiguousarray(np.transpose(L0_xattn_x_proj_w)),
        dtprojT=np.ascontiguousarray(np.transpose(L0_xattn_dt_proj_w)),
        factors=np.ascontiguousarray(L0_ffn_factors),
        ffn_bias=np.ascontiguousarray(L0_ffn_bias),
        identity=np.eye(P, dtype=np.float32),
    )
    nc = bacc.Bacc("TRN2", target_bir_lowering=False, num_devices=1)
    args = [nc.dram_tensor(n, arrays[n].shape, mybir.dt.from_np(arrays[n].dtype), kind="ExternalInput").ap()
            for n in _INS]
    out = nc.dram_tensor("out", x.shape, F32, kind="ExternalOutput").ap()
    ssm_ffn_kernel(nc, *args, out)
    r = run_bass_kernel_spmd(nc, [arrays], core_ids=[0])
    return r.results[0]["out"]
```
